# Optimizing a Trainium2 kernel written in Bass

```python
import numpy as np
import jax
import jax.numpy as jnp

def _softmax(x, axis=-1):
    return jax.nn.softmax(x, axis=axis)

def _gelu(x):
    return jax.nn.gelu(x, approximate=True)

def _silu(x):
    return jax.nn.silu(x)

def _sigmoid(x):
    return jax.nn.sigmoid(x)

def _layernorm(x, axis=-1, eps=1e-05):
    m = jnp.mean(x, axis=axis, keepdims=True)
    v = jnp.var(x, axis=axis, keepdims=True)
    return (x - m) / jnp.sqrt(v + eps)

def _scatter_add(tgt, idx, src, axis=0):
    return tgt.at[idx].add(src)

def _segment_sum(src, seg, n):
    return jax.ops.segment_sum(src, seg, n)
kernel_name = 'mk_adj_seq_d2_adj_r2_4a5931'

def setup_inputs(seed: int=0):
    np.random.seed(seed)
    _w = jnp.asarray

    def _rec_inputs():
        import jax
        import jax.numpy as jnp
        _gk = jax.random.key(seed)
        x = 7.22e-05 + 1 * jax.random.normal(jax.random.fold_in(_gk, 1), (32, 256, 256), jnp.float32)
        _a = jax.random.bernoulli(jax.random.fold_in(_gk, 2), 0.0078125, (32, 256, 256))
        _a = jnp.logical_or(_a, jnp.eye(256, dtype=bool))
        _af = _a.astype(jnp.float32)
        adj = _af
        return (x, adj)
    x, adj = _rec_inputs()

    def _L0_gnn_setup():
        import jax, jax.numpy as jnp
        import numpy as np
        NUM_HID = 256
        BS, N = (8, 1024)
        NEG_BIG = -1000000000.0
        LEAKY_SLOPE = 0.01
        key = jax.random.key(seed)
        k_feats, k_adj, k_w, k_wq, k_wk = jax.random.split(key, 5)
        feats = jax.random.normal(k_feats, (BS, N, NUM_HID), dtype=jnp.float32)
        adj = (jax.random.uniform(k_adj, (BS, N, N)) < 0.05).astype(jnp.float32)
        eye = jnp.eye(N, dtype=jnp.float32)[None]
        adj_mat = jnp.maximum(adj, eye)
        s = 1.0 / np.sqrt(NUM_HID)
        W_fc = jax.random.uniform(k_w, (NUM_HID, NUM_HID), minval=-s, maxval=s, dtype=jnp.float32)
        b_fc = jnp.zeros((NUM_HID,), dtype=jnp.float32)
        w_q = jax.random.uniform(k_wq, (NUM_HID, 1), minval=-s, maxval=s, dtype=jnp.float32)
        b_q = jnp.zeros((1,), dtype=jnp.float32)
        w_k = jax.random.uniform(k_wk, (NUM_HID, 1), minval=-s, maxval=s, dtype=jnp.float32)
        b_k = jnp.zeros((1,), dtype=jnp.float32)
        return {'feats': feats, 'adj_mat': adj_mat, 'W_fc': W_fc, 'b_fc': b_fc, 'w_q': w_q, 'b_q': b_q, 'w_k': w_k, 'b_k': b_k}
    _L0_gnn_all = _L0_gnn_setup()
    _L0_gnn_in = {k: v for k, v in _L0_gnn_all.items() if k in ('W_fc', 'b_fc', 'w_q', 'b_q', 'w_k', 'b_k')}
    del _L0_gnn_all

    def _L1_gnn_setup():
        import jax, jax.numpy as jnp
        import numpy as np
        NUM_HEADS = 8
        EPS = 1e-09
        key = jax.random.key(seed)
        ks = jax.random.split(key, 8)
        B, N, D = (2, 1024, 256)
        s = 1.0 / np.sqrt(D)
        x = jax.random.normal(ks[0], (B, N, D), dtype=jnp.float32)
        adjacency = jax.random.uniform(ks[1], (B, N, N), dtype=jnp.float32)
        W_q = jax.random.normal(ks[2], (D, D), dtype=jnp.float32) * s
        W_k = jax.random.normal(ks[3], (D, D), dtype=jnp.float32) * s
        W_v = jax.random.normal(ks[4], (D, D), dtype=jnp.float32) * s
        b_q = jnp.zeros((D,), jnp.float32)
        b_k = jnp.zeros((D,), jnp.float32)
        b_v = jnp.zeros((D,), jnp.float32)
        w_g = jax.random.normal(ks[5], (2 * D,), dtype=jnp.float32) * (1.0 / np.sqrt(2 * D))
        b_g = jnp.zeros((), jnp.float32)
        return {'x': x, 'adjacency': adjacency, 'W_q': W_q, 'b_q': b_q, 'W_k': W_k, 'b_k': b_k, 'W_v': W_v, 'b_v': b_v, 'w_g': w_g, 'b_g': b_g}
    _L1_gnn_all = _L1_gnn_setup()
    _L1_gnn_in = {k: v for k, v in _L1_gnn_all.items() if k in ('W_q', 'b_q', 'W_k', 'b_k', 'W_v', 'b_v', 'w_g', 'b_g')}
    del _L1_gnn_all
    return {'x': x, 'adj': adj, 'L0_gnn_W_fc': _L0_gnn_in['W_fc'], 'L0_gnn_b_fc': _L0_gnn_in['b_fc'], 'L0_gnn_w_q': _L0_gnn_in['w_q'], 'L0_gnn_b_q': _L0_gnn_in['b_q'], 'L0_gnn_w_k': _L0_gnn_in['w_k'], 'L0_gnn_b_k': _L0_gnn_in['b_k'], 'L1_gnn_W_q': _L1_gnn_in['W_q'], 'L1_gnn_b_q': _L1_gnn_in['b_q'], 'L1_gnn_W_k': _L1_gnn_in['W_k'], 'L1_gnn_b_k': _L1_gnn_in['b_k'], 'L1_gnn_W_v': _L1_gnn_in['W_v'], 'L1_gnn_b_v': _L1_gnn_in['b_v'], 'L1_gnn_w_g': _L1_gnn_in['w_g'], 'L1_gnn_b_g': _L1_gnn_in['b_g']}

def reference(x, adj, L0_gnn_W_fc, L0_gnn_b_fc, L0_gnn_w_q, L0_gnn_b_q, L0_gnn_w_k, L0_gnn_b_k, L1_gnn_W_q, L1_gnn_b_q, L1_gnn_W_k, L1_gnn_b_k, L1_gnn_W_v, L1_gnn_b_v, L1_gnn_w_g, L1_gnn_b_g):
    import jax
    import jax.numpy as jnp

    def _L0_gnn_ref(feats, adj_mat, W_fc, b_fc, w_q, b_q, w_k, b_k):
        import jax, jax.numpy as jnp
        import numpy as np
        NUM_HID = 256
        BS, N = (8, 1024)
        NEG_BIG = -1000000000.0
        LEAKY_SLOPE = 0.01
        feat_proj = jnp.einsum('bnd,de->bne', feats, W_fc) + b_fc
        q = jnp.einsum('bnd,do->bno', feat_proj, w_q) + b_q
        k = jnp.einsum('bnd,do->bno', feat_proj, w_k) + b_k
        logits = q + jnp.swapaxes(k, 2, 1)
        masked = logits + (1.0 - adj_mat) * NEG_BIG
        masked = jnp.where(masked >= 0, masked, LEAKY_SLOPE * masked)
        atten = jax.nn.softmax(masked, axis=-1)
        out = jnp.einsum('bnm,bmd->bnd', atten, feat_proj)
        return out + feats

    def _L1_gnn_ref(x, adjacency, W_q, b_q, W_k, b_k, W_v, b_v, w_g, b_g):
        import jax, jax.numpy as jnp
        import numpy as np
        NUM_HEADS = 8
        EPS = 1e-09
        B, N, D = x.shape
        H = NUM_HEADS
        hd = D // H
        Q = (x @ W_q + b_q).reshape(B, N, H, hd)
        K = (x @ W_k + b_k).reshape(B, N, H, hd)
        V = (x @ W_v + b_v).reshape(B, N, H, hd)
        scores = jnp.einsum('bihd,bjhd->bhij', Q, K) / jnp.sqrt(jnp.float32(hd))
        a = x @ w_g[:D]
        c = x @ w_g[D:]
        soul_bias = a[:, :, None] + c[:, None, :] + b_g
        scores = scores + (soul_bias + jnp.log(adjacency + EPS))[:, None, :, :]
        attn = jax.nn.softmax(scores, axis=-1)
        out = jnp.einsum('bhij,bjhd->bihd', attn, V).reshape(B, N, D)
        return out + x
    x = _L0_gnn_ref(x, adj, L0_gnn_W_fc, L0_gnn_b_fc, L0_gnn_w_q, L0_gnn_b_q, L0_gnn_w_k, L0_gnn_b_k)
    x = _L1_gnn_ref(x, adj, L1_gnn_W_q, L1_gnn_b_q, L1_gnn_W_k, L1_gnn_b_k, L1_gnn_W_v, L1_gnn_b_v, L1_gnn_w_g, L1_gnn_b_g)
    return x

_drawn_inputs = setup_inputs


def setup_inputs(seed=0):
    import zlib

    import numpy as np

    out = dict(_drawn_inputs(seed))
    spreads = {'L0_gnn_b_fc': (0.0, 0.1),
     'L1_gnn_b_q': (0.0, 0.312),
     'L1_gnn_b_k': (0.0, 0.8),
     'L1_gnn_b_v': (0.0, 0.1)}
    factors = {}
    for name, (base, spread) in spreads.items():
        noise = np.random.default_rng([zlib.crc32(name.encode()), seed]).standard_normal(out[name].shape)
        drawn = base * np.exp(spread * noise) if base else spread * noise
        out[name] = jnp.asarray(drawn.astype(out[name].dtype))
    for name, factor in factors.items():
        out[name] = (out[name] * factor).astype(out[name].dtype)
    return out
```

```python
from contextlib import ExitStack

import concourse.bass as bass
from concourse import mybir

F32 = mybir.dt.float32
F32R = mybir.dt.float32r
ALU = mybir.AluOpType
ACT = mybir.ActivationFunctionType

P = 128
BATCH, NODES, FEAT = 32, 256, 256
HEADS = 8
HD = FEAT // HEADS
NT = NODES // P
FT = FEAT // P
GROUPS = HEADS // 4
STACK = 3 * HD
RING = 4
LAG = 2
NEG_BIG = -1e9
SLOPE = 0.01
EPS = 1e-9
SCALE = float(HD) ** -0.5
STACK_COPIES = 12


def build(nc, x, adj, W_fc, b_fc, w_q, b_q, w_k, b_k, W_q, b_q1, W_k, b_k1, W_v, b_v, w_g, b_g, out):
    ctx = ExitStack()
    with ctx:
        def sb(name, shape, dt=F32):
            return ctx.enter_context(nc.sbuf_tensor(name, shape, dt))

        def sem(name):
            return ctx.enter_context(nc.semaphore(name))

        def pair(name, shape, dt=F32):
            return [sb(f"{name}{i}", shape, dt) for i in range(2)]

        ident = sb("ident", [P, P])
        W0 = sb("W0", [P, FT, FEAT + 2])
        row_wq = sb("row_wq", [P, FEAT])
        row_wk = sb("row_wk", [P, FEAT])
        row_bfc = sb("row_bfc", [P, FEAT])
        row_bv = sb("row_bv", [P, FEAT])
        junk = sb("junk", [P, FEAT])
        dots = sb("dots", [P, 2])
        bqk = sb("bqk", [P, 2])
        qk_bias = sb("qk_bias", [P, NT, 2])
        bfc_col = sb("bfc_col", [P, FT])
        bq_raw = sb("bq_raw", [P, FT])
        bq_col = sb("bq_col", [P, FT])
        bk_col = sb("bk_col", [P, FT])
        wq_raw = sb("wq_raw", [P, FT, FEAT])
        wk_raw = sb("wk_raw", [P, FT, FEAT])
        wv_raw = sb("wv_raw", [P, FT, FEAT])
        wg_raw = sb("wg_raw", [P, 2, FT])
        bg_raw = sb("bg_raw", [P, 1])
        wq_s = sb("wq_s", [P, FT, FEAT])
        wv_s = sb("wv_s", [P, FT, FEAT + 2])
        wq_hi, wq_lo = sb("wq_hi", [P, FT, FEAT], F32R), sb("wq_lo", [P, FT, FEAT], F32R)
        wk_hi, wk_lo = sb("wk_hi", [P, FT, FEAT], F32R), sb("wk_lo", [P, FT, FEAT], F32R)
        wv_hi, wv_lo = sb("wv_hi", [P, FT, FEAT + 2], F32R), sb("wv_lo", [P, FT, FEAT + 2], F32R)
        ac_bias = sb("ac_bias", [P, NT, 2])
        eps_col = sb("eps_col", [P, 1])

        x_nat = pair("x_nat", [P, NT, FEAT])
        adj_nat = pair("adj_nat", [P, NT, NODES])
        xT = sb("xT", [P, FT, NODES])
        feat = sb("feat", [P, NT, FEAT])
        qk = sb("qk", [P, NT, 2])
        penalty = sb("penalty", [P, NT, NODES])
        masked = sb("masked", [P, NT, NODES])
        top0 = sb("top0", [P, NT])
        top0q = sb("top0q", [P, NT])
        top0s = sb("top0s", [P, NT])
        shift0 = sb("shift0", [P, NT])
        sloped = sb("sloped", [P, NT, NODES])
        leaky = sb("leaky", [P, NT, NODES])
        p0 = sb("p0", [P, NT, NODES])
        sum0 = sb("sum0", [P, NT])
        rec0 = sb("rec0", [P, NT])
        p0n = sb("p0n", [P, NT, NODES])
        p0T = sb("p0T", [P, NT, NODES])
        x1T = sb("x1T", [P, FT, NODES])
        x1_hi = sb("x1_hi", [P, FT, NODES], F32R)
        x1_lo = sb("x1_lo", [P, FT, NODES], F32R)

        logw = pair("logw", [P, NT, NODES])
        x1n = pair("x1n", [P, NT, FEAT])
        q_hi, q_lo = sb("q_hi", [P, GROUPS, NODES], F32R), sb("q_lo", [P, GROUPS, NODES], F32R)
        k_hi, k_lo = sb("k_hi", [P, GROUPS, NODES], F32R), sb("k_lo", [P, GROUPS, NODES], F32R)
        q_stack = pair("q_stack", [P, HEADS, NODES], F32R)
        k_stack = pair("k_stack", [P, HEADS, NODES], F32R)
        V = pair("V", [P, NT, FEAT])
        ac = sb("ac", [P, NT, 2])
        bias = pair("bias", [P, NT, NODES])
        logits = sb("logits", [P, RING, NT, NODES])
        least = sb("least", [P, HEADS, NT])
        e = sb("e", [P, RING, NT, NODES])
        sums = pair("sums", [P, NT, HEADS])
        rec = sb("rec", [P, NT, HEADS])
        eT = sb("eT", [P, HEADS, NT, NODES])
        oT = sb("oT", [P, GROUPS, NODES])
        y = sb("y", [P, NT, FEAT])
        y_out = pair("y_out", [P, NT, FEAT])

        bank = [ctx.enter_context(nc.psum_tensor(f"bank{i}", [P, 512], F32)) for i in range(8)]
        A, B, S0, S1, T0, T1, O, ON = bank
        S, T = (S0, S1), (T0, T1)

        def halves(b):
            return b[:, :].rearrange("p (t n) -> p t n", t=2)

        s_w = sem("weights_loaded")
        s_ident0, s_ident = sem("ident_zeroed"), sem("ident_ready")
        s_w0, s_wsc, s_whi, s_wready = sem("w0_ready"), sem("weights_scaled"), sem("weights_hi"), sem("weights_ready")
        s_dots, s_cols, s_eps = sem("dots_ready"), sem("bias_columns_ready"), sem("eps_ready")
        x_in = [sem(f"x_loaded{i}") for i in range(2)]
        adj_in = [sem(f"adj_loaded{i}") for i in range(2)]
        xT_ps, xT_sb = sem("xT_made"), sem("xT_copied")
        feat_ps, feat_sb, qk_sb = sem("feat_made"), sem("feat_copied"), sem("qk_copied")
        krow_ps, penalty_sb, masked_sb = sem("krow_made"), sem("penalty_ready"), sem("masked_ready")
        shift_a, shift_b, shift_sb = sem("top0q_ready"), sem("top0s_ready"), sem("shift0_ready")
        sloped_sb = sem("sloped_ready")
        leaky_sb, p0_sb, rec0_sb, p0n_sb = sem("leaky_ready"), sem("p0_ready"), sem("rec0_ready"), sem("p0n_ready")
        p0T_ps, p0T_sb, av0_ps = sem("p0T_made"), sem("p0T_copied"), sem("x1_products_made")
        x1T_sb, x1hi_sb, x1lo_sb = sem("x1T_ready"), sem("x1_hi_ready"), sem("x1_lo_ready")
        x1n_ps, x1n_sb = sem("x1n_made"), sem("x1n_ready")
        q_ps, qhi_sb, qlo_sb = sem("q_made"), sem("q_hi_ready"), sem("q_lo_ready")
        k_ps, khi_sb, klo_sb = sem("k_made"), sem("k_hi_ready"), sem("k_lo_ready")
        q_in = [sem(f"q_stacked{i}") for i in range(2)]
        k_in = [sem(f"k_stacked{i}") for i in range(2)]
        v_ps, v_sb, ac_sb, crow_ps = sem("v_made"), sem("v_copied"), sem("ac_ready"), sem("crow_made")
        logw_sb, bias_sb = sem("logw_ready"), sem("bias_ready")
        scores_ps = sem("scores_made")
        logits_sb = sem("logits_ready")
        e_sb = sem("e_ready")
        eT_ps = sem("eT_made")
        eT_act = sem("eT_copied_by_scalar")
        eT_dve = sem("eT_copied_by_vector")
        av_ps, oT_sb = sem("values_made"), sem("oT_copied")
        on_ps, rec_sb, y_sb, yout_sb = sem("out_transposed"), sem("rec_ready"), sem("y_ready"), sem("y_out_ready")
        stored = [sem(f"out_stored{i}") for i in range(2)]

        dve_beat, pool_beat = sem("vector_has_waited"), sem("gpsimd_has_waited")

        def count(i, k, per=1, more=0):
            return i * (2 * per) + (k * per + more)

        def dma_count(i, k, dmas=1):
            return i * (16 * dmas) + 16 * dmas * (k // 2 + 1)

        def take_waits(engine, i, beat):
            if not isinstance(i, int):
                engine.sem_inc(beat, 1)

        def past(i, k, n):
            return not isinstance(i, int) or k >= n

        def over_graphs(engine, step):
            for k in (-3, -2, -1, 0, 1):
                step(0, k)
            pairs = (BATCH - 4) // 2
            with engine.Fori(1, pairs) as i:
                for k in (0, 1):
                    step(i, k)
            for k in range(2 * pairs, BATCH + 1):
                step(0, k)

        def stage(i, k):
            if not isinstance(i, int):
                return True, True, True, True
            return (k >= -2 and k + 2 < BATCH, k >= -1 and k + 1 < BATCH, 0 <= k < BATCH, k >= 1)

        block = ctx.enter_context(nc.Block())

        @block.sync
        def _(sp):
            def feat_rows(w):
                return w.rearrange("(t p) n -> p t n", p=P)

            def col(w):
                return w.rearrange("(t p) -> p t", p=P)

            def row(w):
                return w.partition_broadcast(P)

            loads = [
                (W0[:, :, 0:FEAT], feat_rows(W_fc)),
                (row_wq[:, :], row(w_q.rearrange("d o -> (d o)"))), (row_wk[:, :], row(w_k.rearrange("d o -> (d o)"))),
                (row_bfc[:, :], row(b_fc)), (row_bv[:, :], row(b_v)),
                (bqk[:, 0:1], row(b_q)), (bqk[:, 1:2], row(b_k)),
                (bfc_col[:, :], col(b_fc)), (bq_raw[:, :], col(b_q1)), (bk_col[:, :], col(b_k1)),
                (wq_raw[:, :, :], feat_rows(W_q)), (wk_raw[:, :, :], feat_rows(W_k)), (wv_raw[:, :, :], feat_rows(W_v)),
                (wg_raw[:, :, :], w_g.rearrange("(a t p) -> p a t", a=2, p=P)),
                (bg_raw[:, :], row(b_g)),
            ]
            assert len(loads) == LOADS
            with nc.allow_non_contiguous_dma(reason="bias columns"):
                for dst, src in loads:
                    sp.dma_start(dst, src).then_inc(s_w, 16)

            def stack(dst, parts, done):
                for n, part in enumerate(parts):
                    for r in range(4):
                        d = dst[HD * n:HD * n + HD, :, :].rearrange("p (g r) n -> p g r n", r=4)[:, :, r, :]
                        sp.dma_start(d.bitcast(F32), part[HD * r:HD * r + HD, :, :].bitcast(F32)).then_inc(done, 16)

            def step(i, k):
                front, proj, heads, rest = stage(i, k)
                if not isinstance(i, int) or 0 <= k + 3 < BATCH:
                    b = i * 2 + (k + 3)
                    if past(i, k + 3, 2):
                        sp.wait_ge(xT_ps, count(i, k + 2))
                    sp.dma_start(x_nat[(k + 3) % 2][:, :, :],
                                 x[bass.ds(b, 1), :, :].rearrange("b (t p) n -> p (b t) n", p=P)).then_inc(x_in[(k + 3) % 2], 16)
                    if past(i, k + 3, 2):
                        sp.wait_ge(penalty_sb, count(i, k + 2))
                        sp.wait_ge(logw_sb, count(i, k + 2))
                    sp.dma_start(adj_nat[(k + 3) % 2][:, :, :],
                                 adj[bass.ds(b, 1), :, :].rearrange("b (t p) n -> p (b t) n", p=P)).then_inc(adj_in[(k + 3) % 2], 16)
                if proj:
                    sp.wait_ge(qlo_sb, count(i, k + 2))
                    sp.wait_ge(qhi_sb, count(i, k + 2))
                    stack(q_stack[(k + 1) % 2], (q_hi, q_lo, q_hi), q_in[(k + 1) % 2])
                    sp.wait_ge(klo_sb, count(i, k + 2))
                    sp.wait_ge(khi_sb, count(i, k + 2))
                    stack(k_stack[(k + 1) % 2], (k_hi, k_hi, k_lo), k_in[(k + 1) % 2])
                if rest:
                    sp.wait_ge(yout_sb, count(i, k))
                    sp.dma_start(out[bass.ds(i * 2 + (k - 1), 1), :, :].rearrange("b (t p) n -> p (b t) n", p=P),
                                 y_out[(k - 1) % 2][:, :, :]).then_inc(stored[(k - 1) % 2], 16)

            over_graphs(sp, step)
            for half in stored:
                sp.wait_ge(half, 16 * BATCH // 2)

        @block.gpsimd
        def _(pool):
            nc.gpsimd.memset(ident[:, :], 0.0).then_inc(s_ident0, 1)
            nc.gpsimd.memset(eps_col[:, :], EPS).then_inc(s_eps, 1)
            nc.gpsimd.memset(ac_bias[:, :, :], 0.0).then_inc(s_eps, 1)
            pool.wait_ge(s_ident0, 1)
            nc.gpsimd.affine_select(out=ident[:, :], in_=ident[:, :], compare_op=ALU.not_equal, fill=1.0,
                                    base=0, pattern=[[-1, P]], channel_multiplier=1).then_inc(s_ident, 1)

            def step(i, k):
                front, proj, heads, rest = stage(i, k)
                if front:
                    if past(i, k + 2, 1):
                        pool.wait_ge(masked_sb, count(i, k + 2))
                    pool.wait_ge(adj_in[k % 2], dma_count(i, k + 2))
                    take_waits(pool, i, pool_beat)
                    nc.gpsimd.tensor_scalar(penalty[:, :, :], adj_nat[k % 2][:, :, :], -1.0, -NEG_BIG,
                                            ALU.add, ALU.mult).then_inc(penalty_sb, 1)
                if rest:
                    pool.wait_ge(y_sb, count(i, k))
                    pool.wait_ge(x1n_sb, count(i, k))
                    if past(i, k - 1, 2):
                        pool.wait_ge(stored[k % 2], dma_count(i, k - 2))
                    nc.gpsimd.tensor_tensor(y_out[(k - 1) % 2][:, :, :], y[:, :, :], x1n[(k - 1) % 2][:, :, :],
                                            ALU.add).then_inc(yout_sb, 1)
                if front:
                    pool.wait_ge(masked_sb, count(i, k + 3))
                    pool.wait_ge(qk_sb, count(i, k + 3))
                    take_waits(pool, i, pool_beat)
                    for t in range(NT):
                        op = nc.gpsimd.tensor_scalar(sloped[:, t, :], masked[:, t, :], qk[:, t, 0:1], SLOPE, ALU.add, ALU.mult)
                    op.then_inc(sloped_sb, 1)
                    if past(i, k + 2, 1):
                        pool.wait_ge(p0T_ps, count(i, k + 2))
                    pool.wait_ge(rec0_sb, count(i, k + 3))
                    pool.wait_ge(p0_sb, count(i, k + 3))
                    take_waits(pool, i, pool_beat)
                    for t in range(NT):
                        op = nc.gpsimd.tensor_scalar(p0n[:, t, :], p0[:, t, :], rec0[:, t:t + 1], None, ALU.mult)
                    op.then_inc(p0n_sb, 1)
                    pool.wait_ge(x1T_sb, count(i, k + 3))
                    take_waits(pool, i, pool_beat)
                    nc.gpsimd.tensor_copy(x1_hi[:, :, :], x1T[:, :, :]).then_inc(x1hi_sb, 1)
                    pool.wait_ge(x1hi_sb, count(i, k + 3))
                    nc.gpsimd.tensor_tensor(x1_lo[:, :, :], x1T[:, :, :], x1_hi[:, :, :].bitcast(F32),
                                            ALU.subtract).then_inc(x1lo_sb, 1)

            over_graphs(pool, step)

        @block.scalar
        def _(act):
            act.wait_ge(s_w, 16 * LOADS)
            nc.scalar.mul(wq_s[:, :, :], wq_raw[:, :, :], -SCALE).then_inc(s_wsc, 1)
            nc.scalar.mul(bq_col[:, :], bq_raw[:, :], -SCALE).then_inc(s_cols, 1)
            nc.scalar.copy(wv_s[:, :, 0:FEAT], wv_raw[:, :, :]).then_inc(s_wsc, 1)
            nc.scalar.mul(wv_s[:, :, FEAT:FEAT + 2], wg_raw[:, :, :].rearrange("p a t -> p t a"), -1.0).then_inc(s_wsc, 1)
            act.wait_ge(s_eps, 2)
            for t in range(NT):
                op = nc.scalar.mul(ac_bias[:, t, 0:1], bg_raw[:, :], -1.0)
            op.then_inc(s_cols, 1)
            act.wait_ge(s_wsc, 3)
            nc.scalar.copy(wq_hi[:, :, :], wq_s[:, :, :]).then_inc(s_whi, 1)
            nc.scalar.copy(wk_hi[:, :, :], wk_raw[:, :, :]).then_inc(s_whi, 1)
            nc.scalar.copy(wv_hi[:, :, :], wv_s[:, :, :]).then_inc(s_whi, 1)
            act.wait_ge(s_cols, 3)

            def exps(i, k, h):
                act.wait_ge(logits_sb, count(i, k, HEADS, h + 1))
                if past(i, k, 1) or h >= RING:
                    act.wait_ge(eT_ps, count(i, k, HEADS, h + 1 - RING))
                for t in range(NT):
                    op = nc.scalar.activation(e[:, h % RING, t, :], logits[:, h % RING, t, :], ACT.Exp,
                                              bias=least[:, h, t:t + 1], scale=-1.0, accum_out=sums[k % 2][:, t, h:h + 1])
                op.then_inc(e_sb, 1)

            def copy_eT(i, k, h):
                act.wait_ge(eT_ps, count(i, k, HEADS, h + 1))
                nc.scalar.copy(eT[:, h, :, :], halves(T[h % 2])).then_inc(eT_act, 1)

            def copy_oT(i, k, g):
                act.wait_ge(av_ps, count(i, k, GROUPS, g + 1))
                if g == 0 and past(i, k, 1):
                    act.wait_ge(on_ps, count(i, k))
                nc.scalar.copy(oT[:, g, :], halves(O)[:, g, :]).then_inc(oT_sb, 1)

            def step(i, k):
                front, proj, heads, rest = stage(i, k)
                if rest:
                    copy_oT(i, k - 1, 1)
                if front:
                    act.wait_ge(xT_ps, count(i, k + 3))
                    nc.scalar.copy(xT[:, :, :], halves(A)).then_inc(xT_sb, 1)
                if heads:
                    exps(i, k, 0)
                if proj:
                    act.wait_ge(q_ps, count(i, k + 2))
                    for g in range(GROUPS):
                        op = nc.scalar.activation(q_hi[:, g, :], halves(B)[:, g, :], ACT.Identity, bias=bq_col[:, g:g + 1])
                    op.then_inc(qhi_sb, 1)
                if heads:
                    exps(i, k, 1)
                if front:
                    act.wait_ge(feat_ps, count(i, k + 3))
                    for t, half in enumerate((A, B)):
                        op = nc.scalar.copy(feat[:, t, :], half[:, 0:FEAT])
                    op.then_inc(feat_sb, 1)
                if heads:
                    copy_eT(i, k, 0)
                    exps(i, k, 2)
                if proj:
                    act.wait_ge(k_ps, count(i, k + 2))
                    for g in range(GROUPS):
                        op = nc.scalar.activation(k_hi[:, g, :], halves(B)[:, g, :], ACT.Identity, bias=bk_col[:, g:g + 1])
                    op.then_inc(khi_sb, 1)
                if heads:
                    exps(i, k, 3)
                if heads:
                    copy_eT(i, k, 2)
                    exps(i, k, 4)
                if front:
                    act.wait_ge(shift_sb, count(i, k + 3))
                    act.wait_ge(leaky_sb, count(i, k + 3))
                    for t in range(NT):
                        op = nc.scalar.activation(p0[:, t, :], leaky[:, t, :], ACT.Exp, bias=shift0[:, t:t + 1],
                                                  accum_out=sum0[:, t:t + 1])
                    op.then_inc(p0_sb, 1)
                if heads:
                    exps(i, k, 5)
                if proj:
                    act.wait_ge(v_ps, count(i, k + 2))
                    for t, half in enumerate((A, B)):
                        op = nc.scalar.copy(V[(k + 1) % 2][:, t, :], half[:, 0:FEAT])
                    op.then_inc(v_sb, 1)
                if heads:
                    copy_eT(i, k, 4)
                    exps(i, k, 6)
                    copy_oT(i, k, 0)
                    exps(i, k, 7)
                if front:
                    act.wait_ge(adj_in[k % 2], dma_count(i, k + 2))
                    if past(i, k + 2, 2):
                        act.wait_ge(bias_sb, count(i, k + 1))
                    nc.scalar.activation(logw[k % 2][:, :, :], adj_nat[k % 2][:, :, :], ACT.Ln,
                                         bias=eps_col[:, 0:1]).then_inc(logw_sb, 1)
                if heads:
                    copy_eT(i, k, 6)

            over_graphs(act, step)

        @block.vector
        def _(dve):
            dve.wait_ge(s_w, 16 * LOADS)
            for n, row_w in enumerate((row_wq, row_wk)):
                for t in range(FT):
                    nc.vector.tensor_tensor_reduce(junk[:, :], W0[:, t, 0:FEAT], row_w[:, :], 1.0, 0.0, ALU.mult,
                                                   ALU.add, W0[:, t, FEAT + n:FEAT + n + 1]).then_inc(s_w0, 1)
                    dve.wait_ge(s_w0, 3 * n + t + 1)
                nc.vector.tensor_tensor_reduce(junk[:, :], row_bfc[:, :], row_w[:, :], 1.0, 0.0, ALU.mult, ALU.add,
                                               dots[:, n:n + 1]).then_inc(s_w0, 1)
                dve.wait_ge(s_w0, 3 * n + 3)
            for t in range(NT):
                op = nc.vector.tensor_tensor(qk_bias[:, t, :], dots[:, :], bqk[:, :], ALU.add)
            op.then_inc(s_cols, 1)
            dve.wait_ge(s_whi, 3)
            nc.vector.tensor_tensor(wq_lo[:, :, :], wq_s[:, :, :], wq_hi[:, :, :].bitcast(F32), ALU.subtract).then_inc(s_wready, 1)
            nc.vector.tensor_tensor(wk_lo[:, :, :], wk_raw[:, :, :], wk_hi[:, :, :].bitcast(F32), ALU.subtract).then_inc(s_wready, 1)
            nc.vector.tensor_tensor(wv_lo[:, :, :], wv_s[:, :, :], wv_hi[:, :, :].bitcast(F32), ALU.subtract).then_inc(s_wready, 1)
            dve.wait_ge(s_cols, 3)

            def add_bias(i, k, h):
                if h == 0:
                    dve.wait_ge(bias_sb, count(i, k + 1))
                if past(i, k, 1) or h >= RING:
                    dve.wait_ge(e_sb, count(i, k, HEADS, h + 1 - RING))
                dve.wait_ge(scores_ps, count(i, k, HEADS, h + 1))
                take_waits(dve, i, dve_beat)
                for t in range(NT):
                    op = nc.vector.tensor_tensor_reduce(logits[:, h % RING, t, :], halves(S[h % 2])[:, t, :], bias[k % 2][:, t, :],
                                                        1.0, 3.0e38, ALU.add, ALU.min, least[:, h, t:t + 1])
                op.then_inc(logits_sb, 1)

            def copy_eT(i, k, h):
                dve.wait_ge(eT_ps, count(i, k, HEADS, h + 1))
                nc.vector.tensor_copy(eT[:, h, :, :], halves(T[h % 2])).then_inc(eT_dve, 1)

            def step(i, k):
                front, proj, heads, rest = stage(i, k)
                if rest:
                    dve.wait_ge(e_sb, count(i, k, HEADS))
                    nc.vector.reciprocal(rec[:, :, :], sums[(k - 1) % 2][:, :, :]).then_inc(rec_sb, 1)
                if heads:
                    add_bias(i, k, 0)
                    add_bias(i, k, 1)
                if proj:
                    dve.wait_ge(qhi_sb, count(i, k + 2))
                    for g in range(GROUPS):
                        op = nc.vector.scalar_tensor_tensor(q_lo[:, g, :], halves(B)[:, g, :], bq_col[:, g:g + 1],
                                                            q_hi[:, g, :].bitcast(F32), ALU.add, ALU.subtract)
                    op.then_inc(qlo_sb, 1)
                if heads:
                    add_bias(i, k, 2)
                if front:
                    dve.wait_ge(feat_sb, count(i, k + 3))
                    for t, half in enumerate((A, B)):
                        op = nc.vector.tensor_tensor(qk[:, t, :], half[:, FEAT:FEAT + 2], qk_bias[:, t, :], ALU.add)
                    op.then_inc(qk_sb, 1)
                if rest:
                    dve.wait_ge(on_ps, count(i, k))
                    dve.wait_ge(rec_sb, count(i, k))
                    if past(i, k - 1, 1):
                        dve.wait_ge(yout_sb, count(i, k - 1))
                    nc.vector.tensor_tensor(
                        y[:, :, :].rearrange("p t (h e) -> p (t h) e", e=HD), ON[:, :].rearrange("p (th e) -> p th e", e=HD),
                        rec[:, :, :].rearrange("p t h -> p (t h)").unsqueeze(2).to_broadcast([P, NT * HEADS, HD]),
                        ALU.mult).then_inc(y_sb, 1)
                if heads:
                    add_bias(i, k, 3)
                    copy_eT(i, k, 1)
                if proj:
                    dve.wait_ge(khi_sb, count(i, k + 2))
                    for g in range(GROUPS):
                        op = nc.vector.scalar_tensor_tensor(k_lo[:, g, :], halves(B)[:, g, :], bk_col[:, g:g + 1],
                                                            k_hi[:, g, :].bitcast(F32), ALU.add, ALU.subtract)
                    op.then_inc(klo_sb, 1)
                if front:
                    dve.wait_ge(krow_ps, count(i, k + 3))
                    dve.wait_ge(penalty_sb, count(i, k + 3))
                    take_waits(dve, i, dve_beat)
                    for t in range(NT):
                        op = nc.vector.tensor_tensor_reduce(masked[:, t, :], A[:, 0:NODES], penalty[:, t, :], 1.0, -3.0e38,
                                                            ALU.add, ALU.max, top0[:, t:t + 1])
                    op.then_inc(masked_sb, 1)
                    dve.wait_ge(masked_sb, count(i, k + 3))
                    dve.wait_ge(qk_sb, count(i, k + 3))
                    nc.vector.tensor_tensor(top0q[:, :], top0[:, :], qk[:, :, 0], ALU.add).then_inc(shift_a, 1)
                if heads:
                    add_bias(i, k, 4)
                if front:
                    dve.wait_ge(shift_a, count(i, k + 3))
                    nc.vector.tensor_scalar(top0s[:, :], top0q[:, :], -SLOPE, None, ALU.mult).then_inc(shift_b, 1)
                    dve.wait_ge(shift_b, count(i, k + 3))
                    nc.vector.scalar_tensor_tensor(shift0[:, :], top0q[:, :], -1.0, top0s[:, :],
                                                   ALU.mult, ALU.min).then_inc(shift_sb, 1)
                    dve.wait_ge(sloped_sb, count(i, k + 3))
                    for t in range(NT):
                        op = nc.vector.scalar_tensor_tensor(leaky[:, t, :], masked[:, t, :], qk[:, t, 0:1], sloped[:, t, :],
                                                            ALU.add, ALU.max)
                    op.then_inc(leaky_sb, 1)
                if heads:
                    copy_eT(i, k, 3)
                    add_bias(i, k, 5)
                if front:
                    dve.wait_ge(p0_sb, count(i, k + 3))
                    nc.vector.reciprocal(rec0[:, :], sum0[:, :]).then_inc(rec0_sb, 1)
                if heads:
                    add_bias(i, k, 6)
                if proj:
                    dve.wait_ge(v_sb, count(i, k + 2))
                    for t, half in enumerate((A, B)):
                        op = nc.vector.tensor_tensor(ac[:, t, :], half[:, FEAT:FEAT + 2], ac_bias[:, t, :], ALU.add)
                    op.then_inc(ac_sb, 1)
                if heads:
                    copy_eT(i, k, 5)
                    add_bias(i, k, 7)
                if proj:
                    dve.wait_ge(crow_ps, count(i, k + 2))
                    dve.wait_ge(logw_sb, count(i, k + 2))
                    for t in range(NT):
                        op = nc.vector.scalar_tensor_tensor(bias[(k + 1) % 2][:, t, :], logw[(k + 1) % 2][:, t, :], ac[:, t, 0:1],
                                                            A[:, 0:NODES], ALU.subtract, ALU.add, reverse0=True)
                    op.then_inc(bias_sb, 1)
                if front:
                    dve.wait_ge(p0T_ps, count(i, k + 3))
                    nc.vector.tensor_copy(p0T[:, :, :], halves(B)).then_inc(p0T_sb, 1)
                if heads:
                    copy_eT(i, k, 7)
                if proj:
                    dve.wait_ge(x1n_ps, count(i, k + 2))
                    if past(i, k + 1, 2):
                        dve.wait_ge(yout_sb, count(i, k))
                    for t in range(NT):
                        op = nc.vector.tensor_tensor(x1n[(k + 1) % 2][:, t, :], halves(B)[:, t, :], row_bv[:, :], ALU.add)
                    op.then_inc(x1n_sb, 1)
                if front:
                    dve.wait_ge(av0_ps, count(i, k + 3))
                    if past(i, k + 2, 1):
                        dve.wait_ge(x1lo_sb, count(i, k + 2))
                    for t in range(FT):
                        op = nc.vector.scalar_tensor_tensor(x1T[:, t, :], halves(A)[:, t, :], bfc_col[:, t:t + 1],
                                                            xT[:, t, :], ALU.add, ALU.add)
                    op.then_inc(x1T_sb, 1)

            over_graphs(dve, step)

        @block.tensor
        def _(pe):
            pe.wait_ge(s_ident, 1)
            pe.wait_ge(s_w0, 6)
            pe.wait_ge(s_wready, 3)

            def split_product(dst, left, right, t0, t1):
                terms = [(left[a], right[b], c) for c in range(FT) for a, b in ((0, 0), (0, 1), (1, 0))]
                for n, (l, r, c) in enumerate(terms):
                    op = pe.matmul(dst, l[:, c, t0], r[:, c, t1], start=(n == 0), stop=(n == len(terms) - 1))
                return op

            def scores(i, k, h):
                if h == 0:
                    pe.wait_ge(q_in[k % 2], dma_count(i, k, STACK_COPIES))
                    pe.wait_ge(k_in[k % 2], dma_count(i, k, STACK_COPIES))
                if past(i, k, 1) or h >= 2:
                    pe.wait_ge(logits_sb, count(i, k, HEADS, h - 1))
                for t in range(NT):
                    op = pe.matmul(halves(S[h % 2])[:, t, :], q_stack[k % 2][0:STACK, h, P * t:P * t + P],
                                   k_stack[k % 2][0:STACK, h, :], start=True, stop=True)
                op.then_inc(scores_ps, 1)

            def transposes(i, k, h):
                pe.wait_ge(e_sb, count(i, k, HEADS, h + 1))
                if past(i, k, 1) or h >= 2:
                    pe.wait_ge((eT_act, eT_dve)[h % 2], count(i, k, HEADS // 2, h // 2))
                for j in range(NT):
                    for t in range(NT):
                        op = pe.transpose(halves(T[h % 2])[:, j, P * t:P * t + P], e[:, h % RING, t, P * j:P * j + P], ident[:, :])
                op.then_inc(eT_ps, 1)

            def values(i, k, g):
                pe.wait_ge(eT_act, count(i, k, HEADS // 2, 2 * g + 2))
                pe.wait_ge(eT_dve, count(i, k, HEADS // 2, 2 * g + 2))
                if g == 0 and past(i, k, 1):
                    pe.wait_ge(oT_sb, count(i, k, GROUPS))
                for j in range(NT):
                    for r in range(4):
                        h = 4 * g + r
                        op = pe.matmul(halves(O)[HD * r:HD * r + HD, g, :], V[k % 2][:, j, HD * h:HD * h + HD], eT[:, h, j, :],
                                       start=(j == 0), stop=(j == NT - 1), tile_position=(0, HD * r))
                op.then_inc(av_ps, 1)

            def step(i, k):
                front, proj, heads, rest = stage(i, k)
                if heads:
                    scores(i, k, 0)
                if rest:
                    values(i, k - 1, 1)
                if front:
                    pe.wait_ge(x_in[k % 2], dma_count(i, k + 2))
                    if past(i, k + 2, 1):
                        pe.wait_ge(x1T_sb, count(i, k + 2))
                    for c in range(FT):
                        for t in range(NT):
                            op = pe.transpose(halves(A)[:, c, P * t:P * t + P], x_nat[k % 2][:, t, P * c:P * c + P], ident[:, :])
                    op.then_inc(xT_ps, 1)
                if heads:
                    scores(i, k, 1)
                if proj:
                    pe.wait_ge(x1lo_sb, count(i, k + 2))
                    pe.wait_ge(x1hi_sb, count(i, k + 2))
                    if past(i, k + 1, 1):
                        pe.wait_ge(x1n_sb, count(i, k + 1))
                    for g in range(GROUPS):
                        op = split_product(halves(B)[:, g, :], (wq_hi, wq_lo), (x1_hi, x1_lo), slice(P * g, P * g + P), slice(0, NODES))
                    op.then_inc(q_ps, 1)
                if heads:
                    scores(i, k, 2)
                if rest:
                    pe.wait_ge(oT_sb, count(i, k, GROUPS))
                    if past(i, k - 1, 1):
                        pe.wait_ge(y_sb, count(i, k - 1))
                    for t in range(NT):
                        for g in range(GROUPS):
                            op = pe.transpose(halves(ON)[:, t, P * g:P * g + P], oT[:, g, P * t:P * t + P], ident[:, :])
                    op.then_inc(on_ps, 1)
                if heads:
                    transposes(i, k, 0)
                if front:
                    pe.wait_ge(xT_sb, count(i, k + 3))
                    if proj:
                        pe.wait_ge(qlo_sb, count(i, k + 2))
                    for t, half in enumerate((A, B)):
                        for c in range(FT):
                            op = pe.matmul(half[:, 0:FEAT + 2], xT[:, c, P * t:P * t + P], W0[:, c, :], start=(c == 0), stop=(c == FT - 1))
                    op.then_inc(feat_ps, 1)
                if heads:
                    scores(i, k, 3)
                    transposes(i, k, 1)
                if proj:
                    pe.wait_ge(qlo_sb, count(i, k + 2))
                    if front:
                        pe.wait_ge(qk_sb, count(i, k + 3))
                    for g in range(GROUPS):
                        op = split_product(halves(B)[:, g, :], (wk_hi, wk_lo), (x1_hi, x1_lo), slice(P * g, P * g + P), slice(0, NODES))
                    op.then_inc(k_ps, 1)
                if front:
                    pe.wait_ge(qk_sb, count(i, k + 3))
                    for t in range(NT):
                        op = pe.transpose(A[:, P * t:P * t + P], qk[:, t, 1:2].to_broadcast([P, P]), ident[:, :])
                    op.then_inc(krow_ps, 1)
                if heads:
                    scores(i, k, 4)
                    transposes(i, k, 2)
                    scores(i, k, 5)
                    transposes(i, k, 3)
                if proj:
                    pe.wait_ge(klo_sb, count(i, k + 2))
                    if front:
                        pe.wait_ge(masked_sb, count(i, k + 3))
                    for t, half in enumerate((A, B)):
                        op = split_product(half[:, 0:FEAT + 2], (x1_hi, x1_lo), (wv_hi, wv_lo), slice(P * t, P * t + P), slice(0, FEAT + 2))
                    op.then_inc(v_ps, 1)
                if heads:
                    scores(i, k, 6)
                    transposes(i, k, 4)
                    values(i, k, 0)
                if proj:
                    pe.wait_ge(ac_sb, count(i, k + 2))
                    for t in range(NT):
                        op = pe.transpose(A[:, P * t:P * t + P], ac[:, t, 1:2].to_broadcast([P, P]), ident[:, :])
                    op.then_inc(crow_ps, 1)
                if front:
                    pe.wait_ge(p0n_sb, count(i, k + 3))
                    if proj:
                        pe.wait_ge(ac_sb, count(i, k + 2))
                    for j in range(NT):
                        for t in range(NT):
                            op = pe.transpose(halves(B)[:, j, P * t:P * t + P], p0n[:, t, P * j:P * j + P], ident[:, :])
                    op.then_inc(p0T_ps, 1)
                if heads:
                    scores(i, k, 7)
                    transposes(i, k, 5)
                if proj:
                    if front:
                        pe.wait_ge(p0T_sb, count(i, k + 3))
                    else:
                        pe.wait_ge(ac_sb, count(i, k + 2))
                    for t in range(NT):
                        for c in range(FT):
                            op = pe.transpose(halves(B)[:, t, P * c:P * c + P], x1T[:, c, P * t:P * t + P], ident[:, :])
                    op.then_inc(x1n_ps, 1)
                if heads:
                    transposes(i, k, 6)
                if front:
                    pe.wait_ge(p0T_sb, count(i, k + 3))
                    if proj:
                        pe.wait_ge(bias_sb, count(i, k + 2))
                    for c in range(FT):
                        for j in range(NT):
                            op = pe.matmul(halves(A)[:, c, :], feat[:, j, P * c:P * c + P], p0T[:, j, :], start=(j == 0), stop=(j == NT - 1))
                    op.then_inc(av0_ps, 1)
                if heads:
                    transposes(i, k, 7)

            over_graphs(pe, step)


LOADS = 15

_INS = ["x", "adj", "L0_gnn_W_fc", "L0_gnn_b_fc", "L0_gnn_w_q", "L0_gnn_b_q", "L0_gnn_w_k", "L0_gnn_b_k",
        "L1_gnn_W_q", "L1_gnn_b_q", "L1_gnn_W_k", "L1_gnn_b_k", "L1_gnn_W_v", "L1_gnn_b_v", "L1_gnn_w_g", "L1_gnn_b_g"]


def kernel(**inputs):
    import numpy as np
    import concourse.bacc as bacc
    from concourse.bass_utils import run_bass_kernel_spmd

    nc = bacc.Bacc("TRN2", target_bir_lowering=False, num_devices=1)
    arrays, args = {}, []
    for name in _INS:
        a = np.ascontiguousarray(inputs[name]).reshape(np.shape(inputs[name]) or (1,))
        arrays[f"in_{name}"] = a
        args.append(nc.dram_tensor(f"in_{name}", a.shape, F32, kind="ExternalInput").ap())
    args.append(nc.dram_tensor("out", (BATCH, NODES, FEAT), F32, kind="ExternalOutput").ap())
    build(nc, *args)
    r = run_bass_kernel_spmd(nc, [arrays], core_ids=[0])
    return r.results[0]["out"]
```

```python
from contextlib import ExitStack

import concourse.bass as bass
from concourse import mybir

F32 = mybir.dt.float32
F32R = mybir.dt.float32r
ALU = mybir.AluOpType
ACT = mybir.ActivationFunctionType

P = 128
BATCH, NODES, FEAT = 32, 256, 256
HEADS = 8
HD = FEAT // HEADS
NT = NODES // P
FT = FEAT // P
GROUPS = HEADS // 4
STACK = 3 * HD
RING = 4
NEG_BIG = -1e9
SLOPE = 0.01
EPS = 1e-9
SCALE = float(HD) ** -0.5
STACK_COPIES = 12
Q_HI, Q_LO, K_HI, K_LO = range(4)
STACK_PARTS = ((Q_HI, K_HI), (Q_LO, K_HI), (Q_HI, K_LO))


def build(nc, x, adj, W_fc, b_fc, w_q, b_q, w_k, b_k, W_q, b_q1, W_k, b_k1, W_v, b_v, w_g, b_g, out):
    ctx = ExitStack()
    with ctx:
        def sb(name, shape, dt=F32):
            return ctx.enter_context(nc.sbuf_tensor(name, shape, dt))

        def sem(name):
            return ctx.enter_context(nc.semaphore(name))

        def pair(name, shape, dt=F32):
            return [sb(f"{name}{i}", shape, dt) for i in range(2)]

        ident = sb("ident", [P, P])
        W0 = sb("W0", [P, FT, FEAT + 2])
        row_wq = sb("row_wq", [P, FEAT])
        row_wk = sb("row_wk", [P, FEAT])
        row_bfc = sb("row_bfc", [P, FEAT])
        row_bv = sb("row_bv", [P, FEAT])
        junk = sb("junk", [P, FEAT])
        dots = sb("dots", [P, 2])
        bqk = sb("bqk", [P, 2])
        qk_bias = sb("qk_bias", [P, NT, 2])
        bfc_col = sb("bfc_col", [P, FT])
        bq_raw = sb("bq_raw", [P, FT])
        bq_col = sb("bq_col", [P, FT])
        bk_col = sb("bk_col", [P, FT])
        wq_raw = sb("wq_raw", [P, FT, FEAT])
        wk_raw = sb("wk_raw", [P, FT, FEAT])
        wv_raw = sb("wv_raw", [P, FT, FEAT])
        wg_raw = sb("wg_raw", [P, 2, FT])
        bg_raw = sb("bg_raw", [P, 1])
        wq_s = sb("wq_s", [P, FT, FEAT])
        wv_s = sb("wv_s", [P, FT, FEAT + 2])
        wq_hi, wq_lo = sb("wq_hi", [P, FT, FEAT], F32R), sb("wq_lo", [P, FT, FEAT], F32R)
        wk_hi, wk_lo = sb("wk_hi", [P, FT, FEAT], F32R), sb("wk_lo", [P, FT, FEAT], F32R)
        wv_hi, wv_lo = sb("wv_hi", [P, FT, FEAT + 2], F32R), sb("wv_lo", [P, FT, FEAT + 2], F32R)
        ac_bias = sb("ac_bias", [P, NT, 2])
        eps_col = sb("eps_col", [P, 1])

        x_nat = pair("x_nat", [P, NT, FEAT])
        adj_nat = pair("adj_nat", [P, NT, NODES])
        xT = pair("xT", [P, FT, NODES])
        feat = pair("feat", [P, NT, FEAT])
        qk = sb("qk", [P, NT, 2])
        penalty = sb("penalty", [P, NT, NODES])
        masked = sb("masked", [P, NT, NODES])
        top0 = sb("top0", [P, NT])
        top0q = sb("top0q", [P, NT])
        top0s = sb("top0s", [P, NT])
        shift0 = sb("shift0", [P, NT])
        sloped = sb("sloped", [P, NT, NODES])
        leaky = sb("leaky", [P, NT, NODES])
        p0 = sb("p0", [P, NT, NODES])
        sum0 = sb("sum0", [P, NT])
        rec0 = sb("rec0", [P, NT])
        p0n = sb("p0n", [P, NT, NODES])
        p0T = sb("p0T", [P, NT, NODES])
        x1T = pair("x1T", [P, FT, NODES])
        x1_hi = pair("x1_hi", [P, FT, NODES], F32R)
        x1_lo = pair("x1_lo", [P, FT, NODES], F32R)

        logw = pair("logw", [P, NT, NODES])
        x1n = pair("x1n", [P, NT, FEAT])
        parts = pair("parts", [P, 4, GROUPS, NODES], F32R)
        stacks = pair("stacks", [P, 4, 2, GROUPS, NODES], F32R)
        V = pair("V", [P, NT, FEAT])
        ac = sb("ac", [P, NT, 2])
        bias = pair("bias", [P, NT, NODES])
        logits = sb("logits", [P, RING, NT, NODES])
        least = sb("least", [P, HEADS, NT])
        e = sb("e", [P, RING, NT, NODES])
        sums = pair("sums", [P, NT, HEADS])
        rec = sb("rec", [P, NT, HEADS])
        eT = sb("eT", [P, HEADS, NT, NODES])
        oT = sb("oT", [P, GROUPS, NODES])
        y = sb("y", [P, NT, FEAT])
        y_out = pair("y_out", [P, NT, FEAT])

        bank = [ctx.enter_context(nc.psum_tensor(f"bank{i}", [P, 512], F32)) for i in range(8)]
        A, B, C, D, S0, S1, T, O = bank
        S = (S0, S1)

        def halves(b):
            return b[:, :].rearrange("p (t n) -> p t n", t=2)

        s_w = sem("weights_loaded")
        s_ident0, s_ident = sem("ident_zeroed"), sem("ident_ready")
        s_w0, s_wsc, s_whi, s_wready = sem("w0_ready"), sem("weights_scaled"), sem("weights_hi"), sem("weights_ready")
        s_cols, s_eps = sem("bias_columns_ready"), sem("eps_ready")
        x_in = [sem(f"x_loaded{i}") for i in range(2)]
        adj_in = [sem(f"adj_loaded{i}") for i in range(2)]
        xT_ps, xT_sb = sem("xT_made"), sem("xT_copied")
        feat_ps, feat_sb, qk_sb = sem("feat_made"), sem("feat_copied"), sem("qk_copied")
        krow_ps, penalty_sb, masked_sb = sem("krow_made"), sem("penalty_ready"), sem("masked_ready")
        shift_a, shift_b, shift_sb = sem("top0q_ready"), sem("top0s_ready"), sem("shift0_ready")
        sloped_sb, leaky_sb = sem("sloped_ready"), sem("leaky_ready")
        p0_sb, rec0_sb, p0n_sb = sem("p0_ready"), sem("rec0_ready"), sem("p0n_ready")
        p0T_ps, p0T_sb, av0_ps = sem("p0T_made"), sem("p0T_copied"), sem("x1_products_made")
        x1T_sb, x1hi_sb, x1lo_sb = sem("x1T_ready"), sem("x1_hi_ready"), sem("x1_lo_ready")
        x1n_ps, x1n_sb = sem("x1n_made"), sem("x1n_ready")
        q_ps, qhi_sb, qlo_sb = sem("q_made"), sem("q_hi_ready"), sem("q_lo_ready")
        k_ps, khi_sb, klo_sb = sem("k_made"), sem("k_hi_ready"), sem("k_lo_ready")
        stacked = [sem(f"parts_stacked{i}") for i in range(2)]
        v_ps, v_sb, ac_sb, crow_ps = sem("v_made"), sem("v_copied"), sem("ac_ready"), sem("crow_made")
        logw_sb, bias_sb = sem("logw_ready"), sem("bias_ready")
        scores_ps = sem("scores_made")
        logits_sb = sem("logits_ready")
        e_sb = sem("e_ready")
        eT_ps = sem("eT_made")
        eT_sb = sem("eT_copied")
        av_ps, oT_sb = sem("values_made"), sem("oT_copied")
        on_ps, rec_sb, y_sb, yout_sb = sem("out_transposed"), sem("rec_ready"), sem("y_ready"), sem("y_out_ready")
        stored = [sem(f"out_stored{i}") for i in range(2)]
        dve_beat, pool_beat, sp_beat = sem("vector_has_waited"), sem("gpsimd_has_waited"), sem("sync_has_waited")

        def count(i, k, per=1, more=0):
            return i * (2 * per) + (k * per + more)

        def dma_count(i, k, dmas=1):
            return i * (16 * dmas) + 16 * dmas * (k // 2 + 1)

        def take_waits(engine, i, beat):
            if not isinstance(i, int):
                engine.sem_inc(beat, 1)

        def has(i, k):
            return not isinstance(i, int) or 0 <= k < BATCH

        def past(i, k, n):
            return not isinstance(i, int) or k >= n

        def over_graphs(engine, step):
            first, last = (DEPTH + 2) // 2, (BATCH - 2) // 2
            for k in range(-1, 2 * first):
                step(0, k)
            with engine.Fori(first, last) as i:
                for k in (0, 1):
                    step(i, k)
            for k in range(2 * last, BATCH + DEPTH):
                step(0, k)

        block = ctx.enter_context(nc.Block())

        @block.sync
        def _(sp):
            def feat_rows(w):
                return w.rearrange("(t p) n -> p t n", p=P)

            def col(w):
                return w.rearrange("(t p) -> p t", p=P)

            def row(w):
                return w.partition_broadcast(P)

            loads = [
                (W0[:, :, 0:FEAT], feat_rows(W_fc)),
                (row_wq[:, :], row(w_q.rearrange("d o -> (d o)"))), (row_wk[:, :], row(w_k.rearrange("d o -> (d o)"))),
                (row_bfc[:, :], row(b_fc)), (row_bv[:, :], row(b_v)),
                (bqk[:, 0:1], row(b_q)), (bqk[:, 1:2], row(b_k)),
                (bfc_col[:, :], col(b_fc)), (bq_raw[:, :], col(b_q1)), (bk_col[:, :], col(b_k1)),
                (wq_raw[:, :, :], feat_rows(W_q)), (wk_raw[:, :, :], feat_rows(W_k)), (wv_raw[:, :, :], feat_rows(W_v)),
                (wg_raw[:, :, :], w_g.rearrange("(a t p) -> p a t", a=2, p=P)),
                (bg_raw[:, :], row(b_g)),
            ]
            assert len(loads) == LOADS
            with nc.allow_non_contiguous_dma(reason="bias columns"):
                for dst, src in loads:
                    sp.dma_start(dst, src).then_inc(s_w, 16)

            def graph_rows(a, i, k):
                return a[bass.ds(i * 2 + k, 1), :, :].rearrange("b (t p) n -> p (b t) n", p=P)

            def load_x(i, k):
                if past(i, k, 2):
                    sp.wait_ge(xT_ps, count(i, k - 1))
                    take_waits(sp, i, sp_beat)
                sp.dma_start(x_nat[k % 2][:, :, :], graph_rows(x, i, k)).then_inc(x_in[k % 2], 16)

            def load_adj(i, k):
                if past(i, k, 2):
                    sp.wait_ge(penalty_sb, count(i, k - 1))
                    take_waits(sp, i, sp_beat)
                    sp.wait_ge(logw_sb, count(i, k - 1))
                    take_waits(sp, i, sp_beat)
                sp.dma_start(adj_nat[k % 2][:, :, :], graph_rows(adj, i, k)).then_inc(adj_in[k % 2], 16)

            def stack(i, k):
                for s in (qhi_sb, qlo_sb, khi_sb, klo_sb):
                    sp.wait_ge(s, count(i, k + 1))
                    take_waits(sp, i, sp_beat)
                if past(i, k, 2):
                    sp.wait_ge(scores_ps, count(i, k - 1, HEADS))
                    take_waits(sp, i, sp_beat)
                for n, (a, b) in enumerate(STACK_PARTS):
                    for r in range(4):
                        dst = stacks[k % 2][HD * n:HD * n + HD, r, :, :, :]
                        src = parts[k % 2][HD * r:HD * r + HD, a:b + 1:b - a, :, :]
                        sp.dma_start(dst.bitcast(F32), src.bitcast(F32)).then_inc(stacked[k % 2], 16)

            def store(i, k):
                sp.wait_ge(yout_sb, count(i, k + 1))
                take_waits(sp, i, sp_beat)
                sp.dma_start(graph_rows(out, i, k), y_out[k % 2][:, :, :]).then_inc(stored[k % 2], 16)

            def step(i, k):
                if has(i, k + 1):
                    load_x(i, k + 1)
                if has(i, k - 5):
                    store(i, k - 5)
                if has(i, k + 1):
                    load_adj(i, k + 1)
                if has(i, k - 2):
                    stack(i, k - 2)

            over_graphs(sp, step)
            for half in stored:
                sp.wait_ge(half, 16 * BATCH // 2)

        @block.gpsimd
        def _(pool):
            nc.gpsimd.memset(ident[:, :], 0.0).then_inc(s_ident0, 1)
            nc.gpsimd.memset(eps_col[:, :], EPS).then_inc(s_eps, 1)
            nc.gpsimd.memset(ac_bias[:, :, :], 0.0).then_inc(s_eps, 1)
            pool.wait_ge(s_ident0, 1)
            nc.gpsimd.affine_select(out=ident[:, :], in_=ident[:, :], compare_op=ALU.not_equal, fill=1.0,
                                    base=0, pattern=[[-1, P]], channel_multiplier=1).then_inc(s_ident, 1)

            def penalize(i, k):
                pool.wait_ge(adj_in[k % 2], dma_count(i, k))
                if past(i, k, 1):
                    pool.wait_ge(masked_sb, count(i, k))
                take_waits(pool, i, pool_beat)
                nc.gpsimd.tensor_scalar(penalty[:, :, :], adj_nat[k % 2][:, :, :], -1.0, -NEG_BIG,
                                        ALU.add, ALU.mult).then_inc(penalty_sb, 1)

            def slope(i, k):
                pool.wait_ge(masked_sb, count(i, k + 1))
                pool.wait_ge(qk_sb, count(i, k + 1))
                if past(i, k, 1):
                    pool.wait_ge(leaky_sb, count(i, k))
                take_waits(pool, i, pool_beat)
                for t in range(NT):
                    op = nc.gpsimd.tensor_scalar(sloped[:, t, :], masked[:, t, :], qk[:, t, 0:1], SLOPE, ALU.add, ALU.mult)
                op.then_inc(sloped_sb, 1)

            def normalize(i, k):
                pool.wait_ge(rec0_sb, count(i, k + 1))
                pool.wait_ge(p0_sb, count(i, k + 1))
                if past(i, k, 1):
                    pool.wait_ge(p0T_ps, count(i, k))
                take_waits(pool, i, pool_beat)
                for t in range(NT):
                    op = nc.gpsimd.tensor_scalar(p0n[:, t, :], p0[:, t, :], rec0[:, t:t + 1], None, ALU.mult)
                op.then_inc(p0n_sb, 1)

            def split_x1(i, k):
                pool.wait_ge(x1T_sb, count(i, k + 1))
                if past(i, k, 2):
                    pool.wait_ge(v_ps, count(i, k - 1))
                take_waits(pool, i, pool_beat)
                nc.gpsimd.tensor_copy(x1_hi[k % 2][:, :, :], x1T[k % 2][:, :, :]).then_inc(x1hi_sb, 1)
                pool.wait_ge(x1hi_sb, count(i, k + 1))
                nc.gpsimd.tensor_tensor(x1_lo[k % 2][:, :, :], x1T[k % 2][:, :, :], x1_hi[k % 2][:, :, :].bitcast(F32),
                                        ALU.subtract).then_inc(x1lo_sb, 1)

            def add_x1(i, k):
                pool.wait_ge(y_sb, count(i, k + 1))
                pool.wait_ge(x1n_sb, count(i, k + 1))
                if past(i, k, 2):
                    pool.wait_ge(stored[k % 2], dma_count(i, k - 2))
                nc.gpsimd.tensor_tensor(y_out[k % 2][:, :, :], y[:, :, :], x1n[k % 2][:, :, :], ALU.add).then_inc(yout_sb, 1)

            def step(i, k):
                if has(i, k - 2):
                    split_x1(i, k - 2)
                if has(i, k - 1):
                    normalize(i, k - 1)
                if has(i, k - 5):
                    add_x1(i, k - 5)
                if has(i, k):
                    penalize(i, k)
                    slope(i, k)

            over_graphs(pool, step)

        @block.scalar
        def _(act):
            nc.scalar.preload_act_table_set("natural_log_exp_and_others")
            act.wait_ge(s_w, 16 * LOADS)
            nc.scalar.mul(wq_s[:, :, :], wq_raw[:, :, :], -SCALE).then_inc(s_wsc, 1)
            nc.scalar.mul(bq_col[:, :], bq_raw[:, :], -SCALE).then_inc(s_cols, 1)
            nc.scalar.copy(wv_s[:, :, 0:FEAT], wv_raw[:, :, :]).then_inc(s_wsc, 1)
            nc.scalar.mul(wv_s[:, :, FEAT:FEAT + 2], wg_raw[:, :, :].rearrange("p a t -> p t a"), -1.0).then_inc(s_wsc, 1)
            act.wait_ge(s_eps, 2)
            for t in range(NT):
                op = nc.scalar.mul(ac_bias[:, t, 0:1], bg_raw[:, :], -1.0)
            op.then_inc(s_cols, 1)
            act.wait_ge(s_wsc, 3)
            nc.scalar.copy(wq_hi[:, :, :], wq_s[:, :, :]).then_inc(s_whi, 1)
            nc.scalar.copy(wk_hi[:, :, :], wk_raw[:, :, :]).then_inc(s_whi, 1)
            nc.scalar.copy(wv_hi[:, :, :], wv_s[:, :, :]).then_inc(s_whi, 1)
            act.wait_ge(s_cols, 3)

            def copy_xT(i, k):
                act.wait_ge(xT_ps, count(i, k + 1))
                if past(i, k, 2):
                    act.wait_ge(x1T_sb, count(i, k - 1))
                nc.scalar.copy(xT[k % 2][:, :, :], halves(C)).then_inc(xT_sb, 1)

            def copy_feat(i, k):
                act.wait_ge(qk_sb, count(i, k + 1))
                if past(i, k, 2):
                    act.wait_ge(av0_ps, count(i, k - 1))
                for t, half in enumerate((B, C)):
                    op = nc.scalar.copy(feat[k % 2][:, t, :], half[:, 0:FEAT])
                op.then_inc(feat_sb, 1)

            def exp0(i, k):
                act.wait_ge(shift_sb, count(i, k + 1))
                act.wait_ge(leaky_sb, count(i, k + 1))
                if past(i, k, 1):
                    act.wait_ge(p0n_sb, count(i, k))
                for t in range(NT):
                    op = nc.scalar.activation(p0[:, t, :], leaky[:, t, :], ACT.Exp, bias=shift0[:, t:t + 1],
                                              accum_out=sum0[:, t:t + 1])
                op.then_inc(p0_sb, 1)

            def log_adj(i, k):
                act.wait_ge(adj_in[k % 2], dma_count(i, k))
                if past(i, k, 2):
                    act.wait_ge(bias_sb, count(i, k - 1))
                nc.scalar.activation(logw[k % 2][:, :, :], adj_nat[k % 2][:, :, :], ACT.Ln,
                                     bias=eps_col[:, 0:1]).then_inc(logw_sb, 1)

            def hi(i, k, made, bank, bias_col, part, done):
                act.wait_ge(made, count(i, k + 1))
                if past(i, k, 2):
                    act.wait_ge(stacked[k % 2], dma_count(i, k - 2, STACK_COPIES))
                for g in range(GROUPS):
                    op = nc.scalar.activation(parts[k % 2][:, part, g, :], halves(bank)[:, g, :], ACT.Identity, bias=bias_col[:, g:g + 1])
                op.then_inc(done, 1)

            def copy_v(i, k):
                act.wait_ge(ac_sb, count(i, k + 1))
                if past(i, k, 2):
                    act.wait_ge(av_ps, count(i, k - 1, GROUPS))
                for t, half in enumerate((A, B)):
                    op = nc.scalar.copy(V[k % 2][:, t, :], half[:, 0:FEAT])
                op.then_inc(v_sb, 1)

            def exp(i, k, h):
                act.wait_ge(logits_sb, count(i, k, HEADS, h + 1))
                if past(i, k, 1) or h >= RING:
                    act.wait_ge(eT_ps, count(i, k, HEADS, h + 1 - RING))
                if h == 0 and past(i, k, 2):
                    act.wait_ge(rec_sb, count(i, k - 1))
                for t in range(NT):
                    op = nc.scalar.activation(e[:, h % RING, t, :], logits[:, h % RING, t, :], ACT.Exp,
                                              bias=least[:, h, t:t + 1], scale=-1.0, accum_out=sums[k % 2][:, t, h:h + 1])
                op.then_inc(e_sb, 1)

            def copy_eT(i, k, h):
                act.wait_ge(eT_ps, count(i, k, HEADS, h + 1))
                if past(i, k, 1):
                    act.wait_ge(av_ps, count(i, k - 1, GROUPS, h // 4 + 1))
                nc.scalar.copy(eT[:, h, :, :], halves(T)).then_inc(eT_sb, 1)

            def copy_oT(i, k, g):
                act.wait_ge(av_ps, count(i, k, GROUPS, g + 1))
                if g == 0 and past(i, k, 1):
                    act.wait_ge(on_ps, count(i, k))
                nc.scalar.copy(oT[:, g, :], halves(O)[:, g, :]).then_inc(oT_sb, 1)

            def step(i, k):
                if has(i, k - 4):
                    exp(i, k - 4, 3)
                if has(i, k - 5):
                    copy_oT(i, k - 5, 1)
                if has(i, k - 4):
                    copy_eT(i, k - 4, 2)
                if has(i, k - 4):
                    exp(i, k - 4, 4)
                if has(i, k - 3):
                    copy_v(i, k - 3)
                if has(i, k - 1):
                    exp0(i, k - 1)
                if has(i, k - 4):
                    exp(i, k - 4, 5)
                if has(i, k):
                    copy_xT(i, k)
                if has(i, k - 4):
                    copy_eT(i, k - 4, 4)
                if has(i, k - 4):
                    exp(i, k - 4, 6)
                if has(i, k - 2):
                    hi(i, k - 2, q_ps, D, bq_col, Q_HI, qhi_sb)
                if has(i, k - 4):
                    exp(i, k - 4, 7)
                if has(i, k):
                    copy_feat(i, k)
                if has(i, k - 1):
                    log_adj(i, k - 1)
                if has(i, k - 4):
                    copy_eT(i, k - 4, 6)
                if has(i, k - 3):
                    exp(i, k - 3, 0)
                if has(i, k - 2):
                    hi(i, k - 2, k_ps, A, bk_col, K_HI, khi_sb)
                if has(i, k - 3):
                    exp(i, k - 3, 1)
                if has(i, k - 4):
                    copy_oT(i, k - 4, 0)
                if has(i, k - 3):
                    copy_eT(i, k - 3, 0)
                if has(i, k - 3):
                    exp(i, k - 3, 2)
                if has(i, k - 3):
                    copy_eT(i, k - 3, 1)
            over_graphs(act, step)

        @block.vector
        def _(dve):
            dve.wait_ge(s_w, 16 * LOADS)
            for n, row_w in enumerate((row_wq, row_wk)):
                for t in range(FT):
                    nc.vector.tensor_tensor_reduce(junk[:, :], W0[:, t, 0:FEAT], row_w[:, :], 1.0, 0.0, ALU.mult,
                                                   ALU.add, W0[:, t, FEAT + n:FEAT + n + 1]).then_inc(s_w0, 1)
                    dve.wait_ge(s_w0, 3 * n + t + 1)
                nc.vector.tensor_tensor_reduce(junk[:, :], row_bfc[:, :], row_w[:, :], 1.0, 0.0, ALU.mult, ALU.add,
                                               dots[:, n:n + 1]).then_inc(s_w0, 1)
                dve.wait_ge(s_w0, 3 * n + 3)
            for t in range(NT):
                op = nc.vector.tensor_tensor(qk_bias[:, t, :], dots[:, :], bqk[:, :], ALU.add)
            op.then_inc(s_cols, 1)
            dve.wait_ge(s_whi, 3)
            nc.vector.tensor_tensor(wq_lo[:, :, :], wq_s[:, :, :], wq_hi[:, :, :].bitcast(F32), ALU.subtract).then_inc(s_wready, 1)
            nc.vector.tensor_tensor(wk_lo[:, :, :], wk_raw[:, :, :], wk_hi[:, :, :].bitcast(F32), ALU.subtract).then_inc(s_wready, 1)
            nc.vector.tensor_tensor(wv_lo[:, :, :], wv_s[:, :, :], wv_hi[:, :, :].bitcast(F32), ALU.subtract).then_inc(s_wready, 1)
            dve.wait_ge(s_cols, 3)

            def copy_qk(i, k):
                dve.wait_ge(feat_ps, count(i, k + 1))
                for t, half in enumerate((B, C)):
                    op = nc.vector.tensor_tensor(qk[:, t, :], half[:, FEAT:FEAT + 2], qk_bias[:, t, :], ALU.add)
                op.then_inc(qk_sb, 1)

            def mask(i, k):
                dve.wait_ge(krow_ps, count(i, k + 1))
                dve.wait_ge(penalty_sb, count(i, k + 1))
                take_waits(dve, i, dve_beat)
                for t in range(NT):
                    op = nc.vector.tensor_tensor_reduce(masked[:, t, :], B[:, 0:NODES], penalty[:, t, :], 1.0, -3.0e38,
                                                        ALU.add, ALU.max, top0[:, t:t + 1])
                op.then_inc(masked_sb, 1)

            def shift(i, k, part):
                if part == 0:
                    dve.wait_ge(masked_sb, count(i, k + 1))
                    dve.wait_ge(qk_sb, count(i, k + 1))
                    nc.vector.tensor_tensor(top0q[:, :], top0[:, :], qk[:, :, 0], ALU.add).then_inc(shift_a, 1)
                if part == 1:
                    dve.wait_ge(shift_a, count(i, k + 1))
                    nc.vector.tensor_scalar(top0s[:, :], top0q[:, :], -SLOPE, None, ALU.mult).then_inc(shift_b, 1)
                if part == 2:
                    dve.wait_ge(shift_b, count(i, k + 1))
                    nc.vector.scalar_tensor_tensor(shift0[:, :], top0q[:, :], -1.0, top0s[:, :],
                                                   ALU.mult, ALU.min).then_inc(shift_sb, 1)

            def leak(i, k):
                dve.wait_ge(sloped_sb, count(i, k + 1))
                for t in range(NT):
                    op = nc.vector.scalar_tensor_tensor(leaky[:, t, :], masked[:, t, :], qk[:, t, 0:1], sloped[:, t, :],
                                                        ALU.add, ALU.max)
                op.then_inc(leaky_sb, 1)

            def reciprocal0(i, k):
                dve.wait_ge(p0_sb, count(i, k + 1))
                nc.vector.reciprocal(rec0[:, :], sum0[:, :]).then_inc(rec0_sb, 1)

            def copy_p0T(i, k):
                dve.wait_ge(p0T_ps, count(i, k + 1))
                nc.vector.tensor_copy(p0T[:, :, :], halves(D)).then_inc(p0T_sb, 1)

            def add_x(i, k):
                dve.wait_ge(av0_ps, count(i, k + 1))
                for t in range(FT):
                    op = nc.vector.scalar_tensor_tensor(x1T[k % 2][:, t, :], halves(D)[:, t, :], bfc_col[:, t:t + 1],
                                                        xT[k % 2][:, t, :], ALU.add, ALU.add)
                op.then_inc(x1T_sb, 1)

            def lo(i, k, hi_done, bank, bias_col, hi_part, lo_part, done):
                dve.wait_ge(hi_done, count(i, k + 1))
                for g in range(GROUPS):
                    op = nc.vector.scalar_tensor_tensor(parts[k % 2][:, lo_part, g, :], halves(bank)[:, g, :], bias_col[:, g:g + 1],
                                                        parts[k % 2][:, hi_part, g, :].bitcast(F32), ALU.add, ALU.subtract)
                op.then_inc(done, 1)

            def copy_ac(i, k):
                dve.wait_ge(v_ps, count(i, k + 1))
                for t, half in enumerate((A, B)):
                    op = nc.vector.tensor_tensor(ac[:, t, :], half[:, FEAT:FEAT + 2], ac_bias[:, t, :], ALU.add)
                op.then_inc(ac_sb, 1)

            def make_bias(i, k):
                dve.wait_ge(crow_ps, count(i, k + 1))
                dve.wait_ge(logw_sb, count(i, k + 1))
                for t in range(NT):
                    op = nc.vector.scalar_tensor_tensor(bias[k % 2][:, t, :], logw[k % 2][:, t, :], ac[:, t, 0:1],
                                                        A[:, 0:NODES], ALU.subtract, ALU.add, reverse0=True)
                op.then_inc(bias_sb, 1)

            def copy_x1n(i, k):
                dve.wait_ge(x1n_ps, count(i, k + 1))
                if past(i, k, 2):
                    dve.wait_ge(yout_sb, count(i, k - 1))
                for t in range(NT):
                    op = nc.vector.tensor_tensor(x1n[k % 2][:, t, :], halves(C)[:, t, :], row_bv[:, :], ALU.add)
                op.then_inc(x1n_sb, 1)

            def logit(i, k, h):
                if h == 0:
                    dve.wait_ge(bias_sb, count(i, k + 1))
                if past(i, k, 1) or h >= RING:
                    dve.wait_ge(e_sb, count(i, k, HEADS, h + 1 - RING))
                dve.wait_ge(scores_ps, count(i, k, HEADS, h + 1))
                take_waits(dve, i, dve_beat)
                for t in range(NT):
                    op = nc.vector.tensor_tensor_reduce(logits[:, h % RING, t, :], halves(S[h % 2])[:, t, :], bias[k % 2][:, t, :],
                                                        1.0, 3.0e38, ALU.add, ALU.min, least[:, h, t:t + 1])
                op.then_inc(logits_sb, 1)

            def copy_eT(i, k, h):
                dve.wait_ge(eT_ps, count(i, k, HEADS, h + 1))
                if past(i, k, 1):
                    dve.wait_ge(av_ps, count(i, k - 1, GROUPS, h // 4 + 1))
                nc.vector.tensor_copy(eT[:, h, :, :], halves(T)).then_inc(eT_sb, 1)

            def reciprocal1(i, k):
                dve.wait_ge(e_sb, count(i, k + 1, HEADS))
                nc.vector.reciprocal(rec[:, :, :], sums[k % 2][:, :, :]).then_inc(rec_sb, 1)

            def divide(i, k):
                dve.wait_ge(on_ps, count(i, k + 1))
                dve.wait_ge(rec_sb, count(i, k + 1))
                if past(i, k, 1):
                    dve.wait_ge(yout_sb, count(i, k))
                nc.vector.tensor_tensor(
                    y[:, :, :].rearrange("p t (h e) -> p (t h) e", e=HD), O[:, :].rearrange("p (th e) -> p th e", e=HD),
                    rec[:, :, :].rearrange("p t h -> p (t h)").unsqueeze(2).to_broadcast([P, NT * HEADS, HD]),
                    ALU.mult).then_inc(y_sb, 1)

            def step(i, k):
                if has(i, k - 4):
                    logit(i, k - 4, 4)
                if has(i, k - 1):
                    shift(i, k - 1, 2)
                if has(i, k - 1):
                    leak(i, k - 1)
                if has(i, k - 4):
                    logit(i, k - 4, 5)
                if has(i, k - 3):
                    copy_ac(i, k - 3)
                if has(i, k - 5):
                    reciprocal1(i, k - 5)
                if has(i, k - 4):
                    copy_eT(i, k - 4, 3)
                if has(i, k - 4):
                    logit(i, k - 4, 6)
                if has(i, k - 1):
                    reciprocal0(i, k - 1)
                if has(i, k - 5):
                    divide(i, k - 5)
                if has(i, k - 4):
                    logit(i, k - 4, 7)
                if has(i, k - 3):
                    make_bias(i, k - 3)
                if has(i, k - 2):
                    lo(i, k - 2, qhi_sb, D, bq_col, Q_HI, Q_LO, qlo_sb)
                if has(i, k - 4):
                    copy_eT(i, k - 4, 5)
                if has(i, k - 3):
                    logit(i, k - 3, 0)
                if has(i, k):
                    copy_qk(i, k)
                if has(i, k - 3):
                    logit(i, k - 3, 1)
                if has(i, k - 1):
                    copy_p0T(i, k - 1)
                if has(i, k - 2):
                    lo(i, k - 2, khi_sb, A, bk_col, K_HI, K_LO, klo_sb)
                if has(i, k - 4):
                    copy_eT(i, k - 4, 7)
                if has(i, k - 3):
                    logit(i, k - 3, 2)
                if has(i, k):
                    mask(i, k)
                if has(i, k - 3):
                    logit(i, k - 3, 3)
                if has(i, k):
                    shift(i, k, 0)
                if has(i, k - 1):
                    add_x(i, k - 1)
                if has(i, k):
                    shift(i, k, 1)
                if has(i, k - 3):
                    copy_x1n(i, k - 3)
            over_graphs(dve, step)

        @block.tensor
        def _(pe):
            pe.wait_ge(s_ident, 1)
            pe.wait_ge(s_w0, 6)
            pe.wait_ge(s_wready, 3)

            def split_product(dst, left, right, t0, t1):
                terms = [(left[a], right[b], c) for c in range(FT) for a, b in ((0, 0), (0, 1), (1, 0))]
                for n, (l, r, c) in enumerate(terms):
                    op = pe.matmul(dst, l[:, c, t0], r[:, c, t1], start=(n == 0), stop=(n == len(terms) - 1))
                return op

            def row_of(dst, column):
                for t in range(NT):
                    op = pe.transpose(dst[:, P * t:P * t + P], column[:, t, 1:2].to_broadcast([P, P]), ident[:, :])
                return op

            def transpose_x(i, k):
                pe.wait_ge(x_in[k % 2], dma_count(i, k))
                if past(i, k, 4):
                    pe.wait_ge(x1n_sb, count(i, k - 3))
                for c in range(FT):
                    for t in range(NT):
                        op = pe.transpose(halves(C)[:, c, P * t:P * t + P], x_nat[k % 2][:, t, P * c:P * c + P], ident[:, :])
                op.then_inc(xT_ps, 1)

            def features(i, k):
                pe.wait_ge(xT_sb, count(i, k + 1))
                if past(i, k, 3):
                    pe.wait_ge(v_sb, count(i, k - 2))
                for t, half in enumerate((B, C)):
                    for c in range(FT):
                        op = pe.matmul(half[:, 0:FEAT + 2], xT[k % 2][:, c, P * t:P * t + P], W0[:, c, :], start=(c == 0), stop=(c == FT - 1))
                op.then_inc(feat_ps, 1)

            def key_row(i, k):
                pe.wait_ge(qk_sb, count(i, k + 1))
                pe.wait_ge(feat_sb, count(i, k + 1))
                row_of(B, qk).then_inc(krow_ps, 1)

            def transpose_p0(i, k):
                pe.wait_ge(p0n_sb, count(i, k + 1))
                if past(i, k, 1):
                    pe.wait_ge(qlo_sb, count(i, k))
                for j in range(NT):
                    for t in range(NT):
                        op = pe.transpose(halves(D)[:, j, P * t:P * t + P], p0n[:, t, P * j:P * j + P], ident[:, :])
                op.then_inc(p0T_ps, 1)

            def combine0(i, k):
                pe.wait_ge(p0T_sb, count(i, k + 1))
                for c in range(FT):
                    for j in range(NT):
                        op = pe.matmul(halves(D)[:, c, :], feat[k % 2][:, j, P * c:P * c + P], p0T[:, j, :], start=(j == 0), stop=(j == NT - 1))
                op.then_inc(av0_ps, 1)

            def queries(i, k):
                pe.wait_ge(x1lo_sb, count(i, k + 1))
                for g in range(GROUPS):
                    op = split_product(halves(D)[:, g, :], (wq_hi, wq_lo), (x1_hi[k % 2], x1_lo[k % 2]), slice(P * g, P * g + P), slice(0, NODES))
                op.then_inc(q_ps, 1)

            def keys(i, k):
                if past(i, k, 1):
                    pe.wait_ge(bias_sb, count(i, k))
                for g in range(GROUPS):
                    op = split_product(halves(A)[:, g, :], (wk_hi, wk_lo), (x1_hi[k % 2], x1_lo[k % 2]), slice(P * g, P * g + P), slice(0, NODES))
                op.then_inc(k_ps, 1)

            def node_values(i, k):
                pe.wait_ge(klo_sb, count(i, k + 1))
                if has(i, k + 2):
                    pe.wait_ge(masked_sb, count(i, k + 3))
                for t, half in enumerate((A, B)):
                    op = split_product(half[:, 0:FEAT + 2], (x1_hi[k % 2], x1_lo[k % 2]), (wv_hi, wv_lo), slice(P * t, P * t + P), slice(0, FEAT + 2))
                op.then_inc(v_ps, 1)

            def c_row(i, k):
                pe.wait_ge(ac_sb, count(i, k + 1))
                pe.wait_ge(v_sb, count(i, k + 1))
                row_of(A, ac).then_inc(crow_ps, 1)

            def transpose_x1(i, k):
                if has(i, k + 3):
                    pe.wait_ge(feat_sb, count(i, k + 4))
                for t in range(NT):
                    for c in range(FT):
                        op = pe.transpose(halves(C)[:, t, P * c:P * c + P], x1T[k % 2][:, c, P * t:P * t + P], ident[:, :])
                op.then_inc(x1n_ps, 1)

            def scores(i, k, h):
                if h == 0:
                    pe.wait_ge(stacked[k % 2], dma_count(i, k, STACK_COPIES))
                if past(i, k, 1) or h >= 2:
                    pe.wait_ge(logits_sb, count(i, k, HEADS, h - 1))
                for t in range(NT):
                    op = pe.matmul(halves(S[h % 2])[:, t, :], stacks[k % 2][0:STACK, h % 4, 0, h // 4, P * t:P * t + P],
                                   stacks[k % 2][0:STACK, h % 4, 1, h // 4, :], start=True, stop=True)
                op.then_inc(scores_ps, 1)

            def transpose_e(i, k, h):
                pe.wait_ge(e_sb, count(i, k, HEADS, h + 1))
                if past(i, k, 1) or h >= 1:
                    pe.wait_ge(eT_sb, count(i, k, HEADS, h))
                for j in range(NT):
                    for t in range(NT):
                        op = pe.transpose(halves(T)[:, j, P * t:P * t + P], e[:, h % RING, t, P * j:P * j + P], ident[:, :])
                op.then_inc(eT_ps, 1)

            def weigh_values(i, k, g):
                pe.wait_ge(eT_sb, count(i, k, HEADS, 4 * g + 4))
                if g == 0 and past(i, k, 1):
                    pe.wait_ge(y_sb, count(i, k))
                if g == 1:
                    pe.wait_ge(oT_sb, count(i, k, GROUPS, 1))
                for j in range(NT):
                    for r in range(4):
                        h = 4 * g + r
                        op = pe.matmul(halves(O)[HD * r:HD * r + HD, g, :], V[k % 2][:, j, HD * h:HD * h + HD], eT[:, h, j, :],
                                       start=(j == 0), stop=(j == NT - 1), tile_position=(0, HD * r))
                op.then_inc(av_ps, 1)

            def transpose_out(i, k):
                pe.wait_ge(oT_sb, count(i, k + 1, GROUPS))
                for t in range(NT):
                    for g in range(GROUPS):
                        op = pe.transpose(halves(O)[:, t, P * g:P * g + P], oT[:, g, P * t:P * t + P], ident[:, :])
                op.then_inc(on_ps, 1)

            def step(i, k):
                if has(i, k - 4):
                    scores(i, k - 4, 5)
                if has(i, k - 4):
                    transpose_e(i, k - 4, 2)
                if has(i, k - 3):
                    node_values(i, k - 3)
                if has(i, k - 4):
                    scores(i, k - 4, 6)
                if has(i, k - 4):
                    transpose_e(i, k - 4, 3)
                if has(i, k - 5):
                    transpose_out(i, k - 5)
                if has(i, k):
                    transpose_x(i, k)
                if has(i, k - 4):
                    scores(i, k - 4, 7)
                if has(i, k - 4):
                    transpose_e(i, k - 4, 4)
                if has(i, k - 3):
                    c_row(i, k - 3)
                if has(i, k - 2):
                    queries(i, k - 2)
                if has(i, k - 3):
                    scores(i, k - 3, 0)
                if has(i, k - 4):
                    transpose_e(i, k - 4, 5)
                if has(i, k):
                    features(i, k)
                if has(i, k - 3):
                    scores(i, k - 3, 1)
                if has(i, k - 4):
                    transpose_e(i, k - 4, 6)
                if has(i, k - 1):
                    transpose_p0(i, k - 1)
                if has(i, k - 2):
                    keys(i, k - 2)
                if has(i, k - 3):
                    scores(i, k - 3, 2)
                if has(i, k - 4):
                    transpose_e(i, k - 4, 7)
                if has(i, k):
                    key_row(i, k)
                if has(i, k - 4):
                    weigh_values(i, k - 4, 0)
                if has(i, k - 3):
                    scores(i, k - 3, 3)
                if has(i, k - 3):
                    transpose_e(i, k - 3, 0)
                if has(i, k - 3):
                    transpose_x1(i, k - 3)
                if has(i, k - 1):
                    combine0(i, k - 1)
                if has(i, k - 3):
                    scores(i, k - 3, 4)
                if has(i, k - 3):
                    transpose_e(i, k - 3, 1)
                if has(i, k - 4):
                    weigh_values(i, k - 4, 1)
            over_graphs(pe, step)


DEPTH = 6
LOADS = 15

_INS = ["x", "adj", "L0_gnn_W_fc", "L0_gnn_b_fc", "L0_gnn_w_q", "L0_gnn_b_q", "L0_gnn_w_k", "L0_gnn_b_k",
        "L1_gnn_W_q", "L1_gnn_b_q", "L1_gnn_W_k", "L1_gnn_b_k", "L1_gnn_W_v", "L1_gnn_b_v", "L1_gnn_w_g", "L1_gnn_b_g"]


def kernel(**inputs):
    import numpy as np
    import concourse.bacc as bacc
    from concourse.bass_utils import run_bass_kernel_spmd

    nc = bacc.Bacc("TRN2", target_bir_lowering=False, num_devices=1)
    arrays, args = {}, []
    for name in _INS:
        a = np.ascontiguousarray(inputs[name]).reshape(np.shape(inputs[name]) or (1,))
        arrays[f"in_{name}"] = a
        args.append(nc.dram_tensor(f"in_{name}", a.shape, F32, kind="ExternalInput").ap())
    args.append(nc.dram_tensor("out", (BATCH, NODES, FEAT), F32, kind="ExternalOutput").ap())
    build(nc, *args)
    r = run_bass_kernel_spmd(nc, [arrays], core_ids=[0])
    return r.results[0]["out"]
```

```python
from contextlib import ExitStack

import concourse.bass as bass
from concourse import mybir

F32 = mybir.dt.float32
F32R = mybir.dt.float32r
ALU = mybir.AluOpType
ACT = mybir.ActivationFunctionType

P = 128
BATCH, NODES, FEAT = 32, 256, 256
HEADS = 8
HD = FEAT // HEADS
NT = NODES // P
FT = FEAT // P
GROUPS = HEADS // 4
STACK = 3 * HD
LAG_B = 3
RING = 4
NEG_BIG = -1e9
SLOPE = 0.01
EPS = 1e-9
SCALE = float(HD) ** -0.5
Q_HI, Q_LO, K_HI, K_LO = range(4)
STACK_PARTS = ((Q_HI, K_HI), (Q_LO, K_HI), (Q_HI, K_LO))


def build(nc, x, adj, W_fc, b_fc, w_q, b_q, w_k, b_k, W_q, b_q1, W_k, b_k1, W_v, b_v, w_g, b_g, out):
    ctx = ExitStack()
    with ctx:
        def sb(name, shape, dt=F32):
            return ctx.enter_context(nc.sbuf_tensor(name, shape, dt))

        def sem(name):
            return ctx.enter_context(nc.semaphore(name))

        def pair(name, shape, dt=F32):
            return [sb(f"{name}{i}", shape, dt) for i in range(2)]

        ident = sb("ident", [P, P])
        W0 = sb("W0", [P, FT, FEAT])
        u_col = sb("u_col", [P, FT, 2])
        u_row = sb("u_row", [P, 2, FEAT])
        W0_hi, W0_lo = sb("W0_hi", [P, FT, FEAT], F32R), sb("W0_lo", [P, FT, FEAT], F32R)
        row_wq = sb("row_wq", [P, FEAT])
        row_wk = sb("row_wk", [P, FEAT])
        row_bfc = sb("row_bfc", [P, FEAT])
        row_bv = sb("row_bv", [P, FEAT])
        dots = sb("dots", [P, 2])
        bqk = sb("bqk", [P, 2])
        qk_bias = sb("qk_bias", [P, NT, 2])
        bq_raw = sb("bq_raw", [P, FT])
        bq_col = sb("bq_col", [P, FT])
        bk_col = sb("bk_col", [P, FT])
        wq_raw = sb("wq_raw", [P, FT, FEAT])
        wk_raw = sb("wk_raw", [P, FT, FEAT])
        wg_raw = sb("wg_raw", [P, 2, FT])
        bg_raw = sb("bg_raw", [P, 1])
        wv_s = sb("wv_s", [P, FT, FEAT + 2])
        wq_hi, wq_lo = sb("wq_hi", [P, FT, FEAT], F32R), sb("wq_lo", [P, FT, FEAT], F32R)
        wk_hi, wk_lo = sb("wk_hi", [P, FT, FEAT], F32R), sb("wk_lo", [P, FT, FEAT], F32R)
        wv_hi, wv_lo = sb("wv_hi", [P, FT, FEAT + 2], F32R), sb("wv_lo", [P, FT, FEAT + 2], F32R)
        ac_bias = sb("ac_bias", [P, NT, 2])
        eps_col = sb("eps_col", [P, 1])

        x_nat = pair("x_nat", [P, NT, FEAT])
        adj_nat = pair("adj_nat", [P, NT, NODES])
        x_hi, x_lo = sb("x_hi", [P, NT, FEAT], F32R), sb("x_lo", [P, NT, FEAT], F32R)
        xb = pair("xb", [P, NT, FEAT])
        terms = sb("terms", [P, 2, NT, FEAT])
        qk_raw = sb("qk_raw", [P, NT, 2])
        qk = sb("qk", [P, NT, 2])
        penalty = sb("penalty", [P, NT, NODES])
        masked = sb("masked", [P, NT, NODES])
        top0 = sb("top0", [P, NT])
        top0q = sb("top0q", [P, NT])
        top0s = sb("top0s", [P, NT])
        shift0 = sb("shift0", [P, NT])
        leaky = sb("leaky", [P, NT, NODES])
        p0 = sb("p0", [P, NT, NODES])
        sum0 = sb("sum0", [P, NT])
        rec0 = sb("rec0", [P, NT])
        p0n = sb("p0n", [P, NT, NODES])
        p0T = sb("p0T", [P, NT, NODES])
        p0T_hi, p0T_lo = sb("p0T_hi", [P, NT, NODES], F32R), sb("p0T_lo", [P, NT, NODES], F32R)
        pxT = sb("pxT", [P, FT, NODES])
        pxT_hi, pxT_lo = sb("pxT_hi", [P, FT, NODES], F32R), sb("pxT_lo", [P, FT, NODES], F32R)
        x1 = pair("x1", [P, NT, FEAT])
        x1T = sb("x1T", [P, FT, NODES])
        x1_hi = pair("x1_hi", [P, FT, NODES], F32R)
        x1_lo = pair("x1_lo", [P, FT, NODES], F32R)

        logw = pair("logw", [P, NT, NODES])
        x1b = pair("x1b", [P, NT, FEAT])
        parts = pair("parts", [P, 4, GROUPS, NODES], F32R)
        stacks = pair("stacks", [P, 4, 2, GROUPS, NODES], F32R)
        V = pair("V", [P, NT, FEAT])
        ac = sb("ac", [P, NT, 2])
        bias = pair("bias", [P, NT, NODES])
        logits = sb("logits", [P, RING, NT, NODES])
        least = sb("least", [P, HEADS, NT])
        e = sb("e", [P, RING, NT, NODES])
        sums = pair("sums", [P, NT, HEADS])
        rec = sb("rec", [P, NT, HEADS])
        eT = sb("eT", [P, HEADS, NT, NODES])
        oT = sb("oT", [P, GROUPS, NODES])
        y_out = pair("y_out", [P, NT, FEAT])

        bank = [ctx.enter_context(nc.psum_tensor(f"bank{i}", [P, 512], F32)) for i in range(8)]
        A, B, C, D, S0, S1, T, O = bank
        S = (S0, S1)

        def halves(b):
            return b[:, :].rearrange("p (t n) -> p t n", t=2)

        s_w, s_b = sem("layer0_weights_loaded"), sem("layer0_biases_loaded")
        s_w1, s_b1 = sem("layer1_weights_loaded"), sem("layer1_biases_loaded")
        s_ident0, s_ident = sem("ident_zeroed"), sem("ident_ready")
        s_ucol, s_urow, s_usb = sem("u_columns_ready"), sem("u_rows_made"), sem("u_rows_copied")
        s_w0hi, s_w0lo = sem("W0_hi_ready"), sem("W0_lo_ready")
        s_wsc, s_whi, s_wready = sem("weights_scaled"), sem("weights_hi"), sem("weights_ready")
        s_qkb, s_cols, s_eps = sem("qk_bias_ready"), sem("bias_columns_ready"), sem("eps_ready")
        x_in = [sem(f"x_loaded{i}") for i in range(2)]
        adj_in = [sem(f"adj_loaded{i}") for i in range(2)]
        dots_sb, qk_sb, xb_sb = sem("dots_ready"), sem("qk_ready"), sem("xb_ready")
        xhi_sb, xlo_sb = sem("x_hi_ready"), sem("x_lo_ready")
        pxT_ps, pxT_sb = sem("pxT_made"), sem("pxT_copied")
        pxhi_sb, pxlo_sb = sem("pxT_hi_ready"), sem("pxT_lo_ready")
        p0hi_sb, p0lo_sb = sem("p0T_hi_ready"), sem("p0T_lo_ready")
        krow_ps, penalty_sb, masked_sb = sem("krow_made"), sem("penalty_ready"), sem("masked_ready")
        shift_a, shift_b, shift_sb = sem("top0q_ready"), sem("top0s_ready"), sem("shift0_ready")
        sloped_sb, leaky_sb = sem("sloped_ready"), sem("leaky_ready")
        p0_sb, rec0_sb, p0n_sb = sem("p0_ready"), sem("rec0_ready"), sem("p0n_ready")
        p0T_ps, p0T_sb, pxw_ps = sem("p0T_made"), sem("p0T_copied"), sem("x1_products_made")
        x1_sb, x1T_ps, x1T_sb = sem("x1_ready"), sem("x1T_made"), sem("x1T_copied")
        x1hi_sb, x1lo_sb = sem("x1_hi_ready"), sem("x1_lo_ready")
        x1b_sb = sem("x1b_ready")
        q_ps, qhi_sb, qlo_sb = sem("q_made"), sem("q_hi_ready"), sem("q_lo_ready")
        k_ps, khi_sb, klo_sb = sem("k_made"), sem("k_hi_ready"), sem("k_lo_ready")
        stacked = [[sem(f"quadrant{r}_stacked{i}") for r in range(4)] for i in range(2)]
        v_ps, v_sb, ac_sb, crow_ps = sem("v_made"), sem("v_copied"), sem("ac_ready"), sem("crow_made")
        logw_sb, bias_sb = sem("logw_ready"), sem("bias_ready")
        scores_ps = sem("scores_made")
        logits_sb = sem("logits_ready")
        e_sb = sem("e_ready")
        eT_ps = sem("eT_made")
        eT_sb = sem("eT_copied")
        av_ps, oT_sb = sem("values_made"), sem("oT_copied")
        on_ps, rec_sb, y_sb, yout_sb = sem("out_transposed"), sem("rec_ready"), sem("y_ready"), sem("y_out_ready")
        stored = [sem(f"out_stored{i}") for i in range(2)]
        dve_beat, pool_beat, sp_beat = sem("vector_has_waited"), sem("gpsimd_has_waited"), sem("sync_has_waited")

        def count(i, k, per=1, more=0):
            return i * (2 * per) + (k * per + more)

        def dma_count(i, k, dmas=1):
            return i * (16 * dmas) + 16 * dmas * (k // 2 + 1)

        def take_waits(engine, i, beat):
            if not isinstance(i, int):
                engine.sem_inc(beat, 1)

        def has(i, k):
            return not isinstance(i, int) or 0 <= k < BATCH

        def past(i, k, n):
            return not isinstance(i, int) or k >= n

        def over_graphs(engine, step, after={}):
            first, last = (DEPTH + 2) // 2, (BATCH - 2) // 2
            for k in range(-1, 2 * first):
                step(0, k)
                if k in after:
                    after[k]()
            with engine.Fori(first, last) as i:
                for k in (0, 1):
                    step(i, k)
            for k in range(2 * last, BATCH + DEPTH):
                step(0, k)

        block = ctx.enter_context(nc.Block())

        @block.sync
        def _(sp):
            def feat_rows(w):
                return w.rearrange("(t p) n -> p t n", p=P)

            def col(w):
                return w.rearrange("(t p) -> p t", p=P)

            def row(w):
                return w.partition_broadcast(P)

            def load_all(loads, done):
                with nc.allow_non_contiguous_dma(reason="bias columns"):
                    for dst, src in loads:
                        sp.dma_start(dst, src).then_inc(done, 16)

            def load_weights():
                layer0 = [
                    (W0[:, :, :], feat_rows(W_fc)),
                    (row_wq[:, :], row(w_q.rearrange("d o -> (d o)"))), (row_wk[:, :], row(w_k.rearrange("d o -> (d o)"))),
                ]
                biases0 = [(row_bfc[:, :], row(b_fc)), (bqk[:, 0:1], row(b_q)), (bqk[:, 1:2], row(b_k))]
                layer1 = [
                    (wk_raw[:, :, :], feat_rows(W_k)), (wq_raw[:, :, :], feat_rows(W_q)),
                    (wv_s[:, :, 0:FEAT], feat_rows(W_v)), (wg_raw[:, :, :], w_g.rearrange("(a t p) -> p a t", a=2, p=P)),
                ]
                assert (len(layer0), len(biases0), len(layer1)) == LOADS[0:3]
                load_all(layer0, s_w)
                load_all(biases0, s_b)
                load_all(layer1, s_w1)

            def load_biases1():
                biases1 = [(bq_raw[:, :], col(b_q1)), (bk_col[:, :], col(b_k1)), (bg_raw[:, :], row(b_g)), (row_bv[:, :], row(b_v))]
                assert len(biases1) == LOADS[3]
                load_all(biases1, s_b1)

            def graph_rows(a, i, k):
                return a[bass.ds(i * 2 + k, 1), :, :].rearrange("b (t p) n -> p (b t) n", p=P)

            def load_x(i, k):
                if past(i, k, 2):
                    sp.wait_ge(qk_sb, count(i, k - 1))
                    take_waits(sp, i, sp_beat)
                    sp.wait_ge(xlo_sb, count(i, k - 1))
                    take_waits(sp, i, sp_beat)
                    sp.wait_ge(xb_sb, count(i, k - 1))
                    take_waits(sp, i, sp_beat)
                sp.dma_start(x_nat[k % 2][:, :, :], graph_rows(x, i, k)).then_inc(x_in[k % 2], 16)

            def load_adj(i, k):
                if past(i, k, 2):
                    sp.wait_ge(penalty_sb, count(i, k - 1))
                    take_waits(sp, i, sp_beat)
                    sp.wait_ge(logw_sb, count(i, k - 1))
                    take_waits(sp, i, sp_beat)
                sp.dma_start(adj_nat[k % 2][:, :, :], graph_rows(adj, i, k)).then_inc(adj_in[k % 2], 16)

            def stack(i, k):
                for s in (qhi_sb, qlo_sb, khi_sb, klo_sb):
                    sp.wait_ge(s, count(i, k + 1))
                    take_waits(sp, i, sp_beat)
                if past(i, k, 2):
                    sp.wait_ge(scores_ps, count(i, k - 1, HEADS))
                    take_waits(sp, i, sp_beat)
                for r in range(4):
                    for n, (a, b) in enumerate(STACK_PARTS):
                        dst = stacks[k % 2][HD * n:HD * n + HD, r, :, :, :]
                        src = parts[k % 2][HD * r:HD * r + HD, a:b + 1:b - a, :, :]
                        sp.dma_start(dst.bitcast(F32), src.bitcast(F32)).then_inc(stacked[k % 2][r], 16)

            def store(i, k):
                sp.wait_ge(yout_sb, count(i, k + 1))
                take_waits(sp, i, sp_beat)
                sp.dma_start(graph_rows(out, i, k), y_out[k % 2][:, :, :]).then_inc(stored[k % 2], 16)

            def step(i, k):
                if has(i, k + 1):
                    load_adj(i, k + 1)
                if has(i, k - 5):
                    store(i, k - 5)
                if has(i, k + 1):
                    load_x(i, k + 1)
                if has(i, k - 2):
                    stack(i, k - 2)
            over_graphs(sp, step, {-1: load_weights, 0: load_biases1})
            for half in stored:
                sp.wait_ge(half, 16 * BATCH // 2)

        @block.gpsimd
        def _(pool):
            nc.gpsimd.memset(ident[:, :], 0.0).then_inc(s_ident0, 1)
            nc.gpsimd.memset(eps_col[:, :], EPS).then_inc(s_eps, 1)
            nc.gpsimd.memset(ac_bias[:, :, :], 0.0).then_inc(s_eps, 1)
            pool.wait_ge(s_ident0, 1)
            nc.gpsimd.affine_select(out=ident[:, :], in_=ident[:, :], compare_op=ALU.not_equal, fill=1.0,
                                    base=0, pattern=[[-1, P]], channel_multiplier=1).then_inc(s_ident, 1)

            def split(whole, hi_part, lo_part, hi_done, lo_done, value):
                nc.gpsimd.tensor_scalar(hi_part[:, :, :], whole[:, :, :], 1.0, 1.0, ALU.mult, ALU.mult).then_inc(hi_done, 1)
                pool.wait_ge(hi_done, value)
                nc.gpsimd.tensor_tensor(lo_part[:, :, :], whole[:, :, :], hi_part[:, :, :].bitcast(F32), ALU.subtract).then_inc(lo_done, 1)

            pool.wait_ge(s_w, 16 * LOADS[0])
            split(W0, W0_hi, W0_lo, s_w0hi, s_w0lo, 1)

            pool.wait_ge(s_whi, 1)
            nc.gpsimd.tensor_tensor(wk_lo[:, :, :], wk_raw[:, :, :], wk_hi[:, :, :].bitcast(F32), ALU.subtract).then_inc(s_wready, 1)

            def penalize(i, k):
                pool.wait_ge(adj_in[k % 2], dma_count(i, k))
                if past(i, k, 1):
                    pool.wait_ge(masked_sb, count(i, k))
                take_waits(pool, i, pool_beat)
                nc.gpsimd.tensor_scalar(penalty[:, :, :], adj_nat[k % 2][:, :, :], -1.0, -NEG_BIG,
                                        ALU.add, ALU.mult).then_inc(penalty_sb, 1)

            def slope(i, k):
                pool.wait_ge(masked_sb, count(i, k + 1))
                pool.wait_ge(qk_sb, count(i, k + 1))
                if past(i, k, 1):
                    pool.wait_ge(p0_sb, count(i, k))
                take_waits(pool, i, pool_beat)
                for t in range(NT):
                    op = nc.gpsimd.tensor_scalar(leaky[:, t, :], masked[:, t, :], qk[:, t, 0:1], SLOPE, ALU.add, ALU.mult)
                op.then_inc(sloped_sb, 1)

            def normalize(i, k):
                pool.wait_ge(rec0_sb, count(i, k + 1))
                pool.wait_ge(p0_sb, count(i, k + 1))
                if past(i, k, 1):
                    pool.wait_ge(p0T_ps, count(i, k))
                take_waits(pool, i, pool_beat)
                for t in range(NT):
                    op = nc.gpsimd.tensor_scalar(p0n[:, t, :], p0[:, t, :], rec0[:, t:t + 1], 1.0, ALU.mult, ALU.mult)
                op.then_inc(p0n_sb, 1)

            def split_x(i, k):
                pool.wait_ge(x_in[k % 2], dma_count(i, k))
                if past(i, k, 1):
                    pool.wait_ge(pxT_ps, count(i, k))
                take_waits(pool, i, pool_beat)
                split(x_nat[k % 2], x_hi, x_lo, xhi_sb, xlo_sb, count(i, k + 1))

            def add_bfc(i, k):
                pool.wait_ge(x_in[k % 2], dma_count(i, k))
                if not past(i, k, 1):
                    pool.wait_ge(s_b, 16 * LOADS[1])
                if past(i, k, 2):
                    pool.wait_ge(x1_sb, count(i, k - 1))
                nc.gpsimd.tensor_tensor(xb[k % 2][:, :, :], x_nat[k % 2][:, :, :], row_bfc[:, :].unsqueeze(1).to_broadcast([P, NT, FEAT]),
                                        ALU.add).then_inc(xb_sb, 1)

            def split_px(i, k):
                pool.wait_ge(pxT_sb, count(i, k + 1))
                if past(i, k, 1):
                    pool.wait_ge(pxw_ps, count(i, k))
                take_waits(pool, i, pool_beat)
                split(pxT, pxT_hi, pxT_lo, pxhi_sb, pxlo_sb, count(i, k + 1))

            def add_bv(i, k):
                pool.wait_ge(x1_sb, count(i, k + 1))
                if not past(i, k, 1):
                    pool.wait_ge(s_b1, 16 * LOADS[3])
                if past(i, k, 2):
                    pool.wait_ge(yout_sb, count(i, k - 1))
                nc.gpsimd.tensor_tensor(x1b[k % 2][:, :, :], x1[k % 2][:, :, :], row_bv[:, :].unsqueeze(1).to_broadcast([P, NT, FEAT]),
                                        ALU.add).then_inc(x1b_sb, 1)

            def split_p0(i, k):
                pool.wait_ge(p0T_sb, count(i, k + 1))
                if past(i, k, 1):
                    pool.wait_ge(pxT_ps, count(i, k))
                take_waits(pool, i, pool_beat)
                split(p0T, p0T_hi, p0T_lo, p0hi_sb, p0lo_sb, count(i, k + 1))

            def split_x1(i, k):
                pool.wait_ge(x1T_sb, count(i, k + 1))
                if past(i, k, 2):
                    pool.wait_ge(v_ps, count(i, k - 1))
                take_waits(pool, i, pool_beat)
                split(x1T, x1_hi[k % 2], x1_lo[k % 2], x1hi_sb, x1lo_sb, count(i, k + 1))

            def add_x1(i, k):
                pool.wait_ge(y_sb, count(i, k + 1))
                pool.wait_ge(x1b_sb, count(i, k + 1))
                nc.gpsimd.tensor_tensor(y_out[k % 2][:, :, :], y_out[k % 2][:, :, :], x1b[k % 2][:, :, :], ALU.add).then_inc(yout_sb, 1)

            def step(i, k):
                if has(i, k - 1):
                    normalize(i, k - 1)
                    split_x(i, k - 1)
                if has(i, k - 5):
                    add_x1(i, k - 5)
                if has(i, k - 1):
                    split_p0(i, k - 1)
                if has(i, k - 2):
                    split_x1(i, k - 2)
                if has(i, k):
                    slope(i, k)
                if has(i, k - 1):
                    add_bfc(i, k - 1)
                    split_px(i, k - 1)
                if has(i, k + 1):
                    penalize(i, k + 1)
                if has(i, k - 3):
                    add_bv(i, k - 3)
            over_graphs(pool, step)

        @block.scalar
        def _(act):
            nc.scalar.preload_act_table_set("natural_log_exp_and_others")
            act.wait_ge(s_eps, 2)

            def prepare():
                act.wait_ge(s_w1, 16 * LOADS[2])
                nc.scalar.copy(wk_hi[:, :, :], wk_raw[:, :, :]).then_inc(s_whi, 1)
                nc.scalar.mul(wq_raw[:, :, :], wq_raw[:, :, :], -SCALE).then_inc(s_wsc, 1)
                nc.scalar.mul(wv_s[:, :, FEAT:FEAT + 2], wg_raw[:, :, :].rearrange("p a t -> p t a"), -1.0).then_inc(s_wsc, 1)
                act.wait_ge(s_wsc, 2)
                nc.scalar.copy(wq_hi[:, :, :], wq_raw[:, :, :]).then_inc(s_whi, 1)
                nc.scalar.copy(wv_hi[:, :, :], wv_s[:, :, :]).then_inc(s_whi, 1)
                act.wait_ge(s_b1, 16 * LOADS[3])
                nc.scalar.mul(bq_col[:, :], bq_raw[:, :], -SCALE).then_inc(s_cols, 1)
                for t in range(NT):
                    op = nc.scalar.mul(ac_bias[:, t, 0:1], bg_raw[:, :], -1.0)
                op.then_inc(s_cols, 1)
                act.wait_ge(s_cols, 2)

            def exp0(i, k):
                act.wait_ge(shift_sb, count(i, k + 1))
                act.wait_ge(leaky_sb, count(i, k + 1))
                if past(i, k, 1):
                    act.wait_ge(p0n_sb, count(i, k))
                for t in range(NT):
                    op = nc.scalar.activation(p0[:, t, :], leaky[:, t, :], ACT.Exp, bias=shift0[:, t:t + 1],
                                              accum_out=sum0[:, t:t + 1])
                op.then_inc(p0_sb, 1)

            def log_adj(i, k):
                act.wait_ge(adj_in[k % 2], dma_count(i, k))
                if past(i, k, 2):
                    act.wait_ge(bias_sb, count(i, k - 1))
                nc.scalar.activation(logw[k % 2][:, :, :], adj_nat[k % 2][:, :, :], ACT.Ln,
                                     bias=eps_col[:, 0:1]).then_inc(logw_sb, 1)

            def hi(i, k, made, bank, bias_col, part, done):
                act.wait_ge(made, count(i, k + 1))
                if past(i, k, 2):
                    act.wait_ge(scores_ps, count(i, k - 2, HEADS, 4))
                for g in range(GROUPS):
                    op = nc.scalar.activation(parts[k % 2][:, part, g, :], halves(bank)[:, g, :], ACT.Identity, bias=bias_col[:, g:g + 1])
                op.then_inc(done, 1)

            def exp(i, k, h):
                act.wait_ge(logits_sb, count(i, k, HEADS, h + 1))
                if past(i, k, 1) or h >= RING:
                    act.wait_ge(eT_ps, count(i, k, HEADS, h + 1 - RING))
                if h == 0 and past(i, k, 2):
                    act.wait_ge(rec_sb, count(i, k - 1))
                for t in range(NT):
                    op = nc.scalar.activation(e[:, h % RING, t, :], logits[:, h % RING, t, :], ACT.Exp,
                                              bias=least[:, h, t:t + 1], scale=-1.0, accum_out=sums[k % 2][:, t, h:h + 1])
                op.then_inc(e_sb, 1)

            def copy_pxT(i, k):
                act.wait_ge(pxT_ps, count(i, k + 1))
                if past(i, k, 1):
                    act.wait_ge(pxlo_sb, count(i, k))
                nc.scalar.copy(pxT[:, :, :], halves(D)).then_inc(pxT_sb, 1)

            def copy_v(i, k):
                act.wait_ge(ac_sb, count(i, k + 1))
                if past(i, k, 2):
                    act.wait_ge(av_ps, count(i, k - 1, GROUPS))
                for t, half in enumerate((A, B)):
                    op = nc.scalar.copy(V[k % 2][:, t, :], half[:, 0:FEAT])
                op.then_inc(v_sb, 1)

            def copy_eT(i, k, h):
                act.wait_ge(eT_ps, count(i, k, HEADS, h + 1))
                if past(i, k, 1):
                    act.wait_ge(av_ps, count(i, k - 1, GROUPS, h // 4 + 1))
                nc.scalar.copy(eT[:, h, :, :], halves(T)).then_inc(eT_sb, 1)

            def copy_oT(i, k, g):
                act.wait_ge(av_ps, count(i, k, GROUPS, g + 1))
                if g == 0 and past(i, k, 1):
                    act.wait_ge(on_ps, count(i, k))
                nc.scalar.copy(oT[:, g, :], halves(O)[:, g, :]).then_inc(oT_sb, 1)

            def copy_p0T(i, k):
                act.wait_ge(p0T_ps, count(i, k + 1))
                if past(i, k, 1):
                    act.wait_ge(p0lo_sb, count(i, k))
                nc.scalar.copy(p0T[:, :, :], halves(D)).then_inc(p0T_sb, 1)

            def step(i, k):
                if has(i, k - 4):
                    exp(i, k - 4, 0)
                if has(i, k - 3):
                    hi(i, k - 3, k_ps, A, bk_col, K_HI, khi_sb)
                if has(i, k - 5):
                    copy_eT(i, k - 5, 7)
                if has(i, k - 4):
                    exp(i, k - 4, 1)
                if has(i, k - 3):
                    hi(i, k - 3, q_ps, C, bq_col, Q_HI, qhi_sb)
                if has(i, k - 1):
                    exp0(i, k - 1)
                if has(i, k - 4):
                    exp(i, k - 4, 2)
                if has(i, k - 5):
                    copy_oT(i, k - 5, 1)
                if has(i, k - 4):
                    copy_eT(i, k - 4, 1)
                    exp(i, k - 4, 3)
                if has(i, k - 3):
                    copy_v(i, k - 3)
                if has(i, k - 4):
                    copy_eT(i, k - 4, 2)
                    exp(i, k - 4, 4)
                if has(i, k - 1):
                    copy_p0T(i, k - 1)
                if has(i, k - 4):
                    exp(i, k - 4, 5)
                    copy_eT(i, k - 4, 4)
                    exp(i, k - 4, 6)
                    copy_eT(i, k - 4, 5)
                    exp(i, k - 4, 7)
                if has(i, k - 1):
                    log_adj(i, k - 1)
                    copy_pxT(i, k - 1)
            over_graphs(act, step, {-1: prepare})

        @block.vector
        def _(dve):
            dve.wait_ge(s_w, 16 * LOADS[0])
            for n, row_w in enumerate((row_wq, row_wk)):
                for t in range(FT):
                    nc.vector.tensor_tensor_reduce(logits[:, n, t, :], W0[:, t, 0:FEAT], row_w[:, :], 1.0, 0.0, ALU.mult,
                                                   ALU.add, u_col[:, t, n:n + 1]).then_inc(s_ucol, 1)
            dve.wait_ge(s_b, 16 * LOADS[1])
            for n, row_w in enumerate((row_wq, row_wk)):
                nc.vector.tensor_tensor_reduce(logits[:, 2 + n, 0, :], row_bfc[:, :], row_w[:, :], 1.0, 0.0, ALU.mult, ALU.add,
                                               dots[:, n:n + 1]).then_inc(s_qkb, 1)
            dve.wait_ge(s_qkb, 2)
            for t in range(NT):
                op = nc.vector.tensor_tensor(qk_bias[:, t, :], dots[:, :], bqk[:, :], ALU.add)
            op.then_inc(s_qkb, 1)
            dve.wait_ge(s_qkb, 3)
            dve.wait_ge(s_urow, 1)
            nc.vector.tensor_copy(u_row[:, :, :], halves(C)).then_inc(s_usb, 1)
            dve.wait_ge(s_usb, 1)

            def prepare():
                dve.wait_ge(s_whi, 3)
                for lo_part, whole, hi_part in ((wq_lo, wq_raw, wq_hi), (wv_lo, wv_s, wv_hi)):
                    nc.vector.tensor_tensor(lo_part[:, :, :], whole[:, :, :], hi_part[:, :, :].bitcast(F32), ALU.subtract).then_inc(s_wready, 1)
                dve.wait_ge(s_cols, 2)
                dve.wait_ge(s_b1, 16 * LOADS[3])

            def dots0(i, k):
                dve.wait_ge(x_in[k % 2], dma_count(i, k))
                take_waits(dve, i, dve_beat)
                for t in range(NT):
                    for n in range(2):
                        op = nc.vector.tensor_tensor_reduce(terms[:, n, t, :], x_nat[k % 2][:, t, :], u_row[:, n, :], 1.0, 0.0,
                                                            ALU.mult, ALU.add, qk_raw[:, t, n:n + 1])
                op.then_inc(dots_sb, 1)

            def make_qk(i, k):
                dve.wait_ge(dots_sb, count(i, k + 1))
                if past(i, k, 1):
                    dve.wait_ge(leaky_sb, count(i, k))
                nc.vector.tensor_tensor(qk[:, :, :], qk_raw[:, :, :], qk_bias[:, :, :], ALU.add).then_inc(qk_sb, 1)

            def mask(i, k):
                dve.wait_ge(krow_ps, count(i, k + 1))
                dve.wait_ge(penalty_sb, count(i, k + 1))
                take_waits(dve, i, dve_beat)
                for t in range(NT):
                    op = nc.vector.tensor_tensor_reduce(masked[:, t, :], B[:, 0:NODES], penalty[:, t, :], 1.0, -3.0e38,
                                                        ALU.add, ALU.max, top0[:, t:t + 1])
                op.then_inc(masked_sb, 1)

            def shift(i, k, part):
                if part == 0:
                    dve.wait_ge(masked_sb, count(i, k + 1))
                    dve.wait_ge(qk_sb, count(i, k + 1))
                    nc.vector.tensor_tensor(top0q[:, :], top0[:, :], qk[:, :, 0], ALU.add).then_inc(shift_a, 1)
                if part == 1:
                    dve.wait_ge(shift_a, count(i, k + 1))
                    nc.vector.tensor_scalar(top0s[:, :], top0q[:, :], -SLOPE, None, ALU.mult).then_inc(shift_b, 1)
                if part == 2:
                    dve.wait_ge(shift_b, count(i, k + 1))
                    if past(i, k, 1):
                        dve.wait_ge(p0_sb, count(i, k))
                    nc.vector.scalar_tensor_tensor(shift0[:, :], top0q[:, :], -1.0, top0s[:, :],
                                                   ALU.mult, ALU.min).then_inc(shift_sb, 1)

            def reciprocal0(i, k):
                dve.wait_ge(p0_sb, count(i, k + 1))
                nc.vector.reciprocal(rec0[:, :], sum0[:, :]).then_inc(rec0_sb, 1)

            def add_x(i, k):
                dve.wait_ge(pxw_ps, count(i, k + 1))
                dve.wait_ge(xb_sb, count(i, k + 1))
                if past(i, k, 2):
                    dve.wait_ge(x1b_sb, count(i, k - 1))
                nc.vector.tensor_tensor(x1[k % 2][:, :, :], halves(C), xb[k % 2][:, :, :], ALU.add).then_inc(x1_sb, 1)

            def lo(i, k, hi_done, bank, bias_col, hi_part, lo_part, done):
                dve.wait_ge(hi_done, count(i, k + 1))
                for g in range(GROUPS):
                    op = nc.vector.scalar_tensor_tensor(parts[k % 2][:, lo_part, g, :], halves(bank)[:, g, :], bias_col[:, g:g + 1],
                                                        parts[k % 2][:, hi_part, g, :].bitcast(F32), ALU.add, ALU.subtract)
                op.then_inc(done, 1)

            def copy_ac(i, k):
                dve.wait_ge(v_ps, count(i, k + 1))
                for t, half in enumerate((A, B)):
                    op = nc.vector.tensor_tensor(ac[:, t, :], half[:, FEAT:FEAT + 2], ac_bias[:, t, :], ALU.add)
                op.then_inc(ac_sb, 1)

            def make_bias(i, k):
                dve.wait_ge(crow_ps, count(i, k + 1))
                dve.wait_ge(logw_sb, count(i, k + 1))
                for t in range(NT):
                    op = nc.vector.scalar_tensor_tensor(bias[k % 2][:, t, :], logw[k % 2][:, t, :], ac[:, t, 0:1],
                                                        A[:, 0:NODES], ALU.subtract, ALU.add, reverse0=True)
                op.then_inc(bias_sb, 1)

            def logit(i, k, h):
                if h == 0:
                    dve.wait_ge(bias_sb, count(i, k + 1))
                if past(i, k, 1) or h >= RING:
                    dve.wait_ge(e_sb, count(i, k, HEADS, h + 1 - RING))
                dve.wait_ge(scores_ps, count(i, k, HEADS, h + 1))
                take_waits(dve, i, dve_beat)
                for t in range(NT):
                    op = nc.vector.tensor_tensor_reduce(logits[:, h % RING, t, :], halves(S[h % 2])[:, t, :], bias[k % 2][:, t, :],
                                                        1.0, 3.0e38, ALU.add, ALU.min, least[:, h, t:t + 1])
                op.then_inc(logits_sb, 1)

            def reciprocal1(i, k):
                dve.wait_ge(e_sb, count(i, k + 1, HEADS))
                if past(i, k, 1):
                    dve.wait_ge(y_sb, count(i, k))
                nc.vector.reciprocal(rec[:, :, :], sums[k % 2][:, :, :]).then_inc(rec_sb, 1)

            def divide(i, k):
                dve.wait_ge(on_ps, count(i, k + 1))
                dve.wait_ge(rec_sb, count(i, k + 1))
                if past(i, k, 2):
                    dve.wait_ge(stored[k % 2], dma_count(i, k - 2))
                nc.vector.tensor_tensor(
                    y_out[k % 2][:, :, :].rearrange("p t (h e) -> p (t h) e", e=HD), O[:, :].rearrange("p (th e) -> p th e", e=HD),
                    rec[:, :, :].rearrange("p t h -> p (t h)").unsqueeze(2).to_broadcast([P, NT * HEADS, HD]),
                    ALU.mult).then_inc(y_sb, 1)

            def copy_x1T(i, k):
                dve.wait_ge(x1T_ps, count(i, k + 1))
                if past(i, k, 1):
                    dve.wait_ge(x1lo_sb, count(i, k))
                nc.vector.tensor_copy(x1T[:, :, :], halves(C)).then_inc(x1T_sb, 1)

            def copy_eT(i, k, h):
                dve.wait_ge(eT_ps, count(i, k, HEADS, h + 1))
                if past(i, k, 1):
                    dve.wait_ge(av_ps, count(i, k - 1, GROUPS, h // 4 + 1))
                nc.vector.tensor_copy(eT[:, h, :, :], halves(T)).then_inc(eT_sb, 1)

            def copy_oT(i, k, g):
                dve.wait_ge(av_ps, count(i, k, GROUPS, g + 1))
                if g == 0 and past(i, k, 1):
                    dve.wait_ge(on_ps, count(i, k))
                nc.vector.tensor_copy(oT[:, g, :], halves(O)[:, g, :]).then_inc(oT_sb, 1)

            def leak(i, k):
                dve.wait_ge(sloped_sb, count(i, k + 1))
                for t in range(NT):
                    op = nc.vector.scalar_tensor_tensor(leaky[:, t, :], masked[:, t, :], qk[:, t, 0:1], leaky[:, t, :],
                                                        ALU.add, ALU.max)
                op.then_inc(leaky_sb, 1)

            def step(i, k):
                if has(i, k - 1):
                    shift(i, k - 1, 2)
                if has(i, k - 4):
                    logit(i, k - 4, 2)
                if has(i, k - 3):
                    lo(i, k - 3, khi_sb, A, bk_col, K_HI, K_LO, klo_sb)
                if has(i, k - 4):
                    copy_eT(i, k - 4, 0)
                if has(i, k - 3):
                    lo(i, k - 3, qhi_sb, C, bq_col, Q_HI, Q_LO, qlo_sb)
                if has(i, k - 4):
                    logit(i, k - 4, 3)
                if has(i, k - 1):
                    reciprocal0(i, k - 1)
                if has(i, k):
                    dots0(i, k)
                if has(i, k - 3):
                    copy_ac(i, k - 3)
                if has(i, k - 4):
                    logit(i, k - 4, 4)
                if has(i, k - 5):
                    divide(i, k - 5)
                if has(i, k - 4):
                    logit(i, k - 4, 5)
                if has(i, k - 2):
                    add_x(i, k - 2)
                if has(i, k - 4):
                    copy_eT(i, k - 4, 3)
                    logit(i, k - 4, 6)
                if has(i, k):
                    make_qk(i, k)
                if has(i, k - 2):
                    copy_x1T(i, k - 2)
                if has(i, k - 4):
                    logit(i, k - 4, 7)
                if has(i, k - 3):
                    make_bias(i, k - 3)
                if has(i, k - 4):
                    copy_oT(i, k - 4, 0)
                if has(i, k):
                    mask(i, k)
                if has(i, k - 3):
                    logit(i, k - 3, 0)
                if has(i, k):
                    shift(i, k, 0)
                if has(i, k - 4):
                    copy_eT(i, k - 4, 6)
                if has(i, k):
                    shift(i, k, 1)
                if has(i, k - 4):
                    reciprocal1(i, k - 4)
                if has(i, k - 3):
                    logit(i, k - 3, 1)
                if has(i, k):
                    leak(i, k)
            over_graphs(dve, step, {1: prepare})

        @block.tensor
        def _(pe):
            pe.wait_ge(s_ident, 1)

            def split_product(dst, left, right, t0, t1):
                terms = [(left[a], right[b], c) for c in range(FT) for a, b in ((0, 0), (0, 1), (1, 0))]
                for n, (l, r, c) in enumerate(terms):
                    op = pe.matmul(dst, l[:, c, t0], r[:, c, t1], start=(n == 0), stop=(n == len(terms) - 1))
                return op

            def row_of(dst, column, n=1):
                for t in range(2):
                    op = pe.transpose(dst[:, P * t:P * t + P], column[:, t, n:n + 1].to_broadcast([P, P]), ident[:, :])
                return op

            pe.wait_ge(s_ucol, 2 * FT)
            for n in range(2):
                op = row_of(halves(C)[:, n, :], u_col, n)
            op.then_inc(s_urow, 1)

            def key_row(i, k):
                pe.wait_ge(qk_sb, count(i, k + 1))
                if past(i, k, LAG_B):
                    pe.wait_ge(v_sb, count(i, k + 1 - LAG_B))
                row_of(B, qk).then_inc(krow_ps, 1)

            def transpose_p0(i, k):
                pe.wait_ge(p0n_sb, count(i, k + 1))
                if past(i, k, 1):
                    pe.wait_ge(pxT_sb, count(i, k))
                for j in range(NT):
                    for t in range(NT):
                        op = pe.transpose(halves(D)[:, j, P * t:P * t + P], p0n[:, t, P * j:P * j + P], ident[:, :])
                op.then_inc(p0T_ps, 1)

            def combine0(i, k):
                pe.wait_ge(p0lo_sb, count(i, k + 1))
                pe.wait_ge(xlo_sb, count(i, k + 1))
                for c in range(FT):
                    op = split_product(halves(D)[:, c, :], (x_hi, x_lo), (p0T_hi, p0T_lo), slice(P * c, P * c + P), slice(0, NODES))
                op.then_inc(pxT_ps, 1)

            def project0(i, k):
                if not past(i, k, 1):
                    pe.wait_ge(s_w0lo, 1)
                    pe.wait_ge(s_usb, 1)
                pe.wait_ge(pxlo_sb, count(i, k + 1))
                if past(i, k, 1):
                    pe.wait_ge(qlo_sb, count(i, k))
                for t in range(NT):
                    op = split_product(halves(C)[:, t, :], (pxT_hi, pxT_lo), (W0_hi, W0_lo), slice(P * t, P * t + P), slice(0, FEAT))
                op.then_inc(pxw_ps, 1)

            def transpose_x1(i, k):
                pe.wait_ge(x1_sb, count(i, k + 1))
                for c in range(FT):
                    for t in range(NT):
                        op = pe.transpose(halves(C)[:, c, P * t:P * t + P], x1[k % 2][:, t, P * c:P * c + P], ident[:, :])
                op.then_inc(x1T_ps, 1)

            def queries(i, k):
                if not past(i, k, 1):
                    pe.wait_ge(s_wready, 3)
                pe.wait_ge(x1lo_sb, count(i, k + 1))
                for g in range(GROUPS):
                    op = split_product(halves(C)[:, g, :], (wq_hi, wq_lo), (x1_hi[k % 2], x1_lo[k % 2]), slice(P * g, P * g + P), slice(0, NODES))
                op.then_inc(q_ps, 1)

            def keys(i, k):
                if not past(i, k, 1):
                    pe.wait_ge(s_wready, 3)
                pe.wait_ge(x1lo_sb, count(i, k + 1))
                if past(i, k, 1):
                    pe.wait_ge(bias_sb, count(i, k))
                for g in range(GROUPS):
                    op = split_product(halves(A)[:, g, :], (wk_hi, wk_lo), (x1_hi[k % 2], x1_lo[k % 2]), slice(P * g, P * g + P), slice(0, NODES))
                op.then_inc(k_ps, 1)

            def node_values(i, k):
                pe.wait_ge(klo_sb, count(i, k + 1))
                if has(i, k + LAG_B - 1):
                    pe.wait_ge(masked_sb, count(i, k + LAG_B))
                for t, half in enumerate((A, B)):
                    op = split_product(half[:, 0:FEAT + 2], (x1_hi[k % 2], x1_lo[k % 2]), (wv_hi, wv_lo), slice(P * t, P * t + P), slice(0, FEAT + 2))
                op.then_inc(v_ps, 1)

            def c_row(i, k):
                pe.wait_ge(ac_sb, count(i, k + 1))
                pe.wait_ge(v_sb, count(i, k + 1))
                row_of(A, ac).then_inc(crow_ps, 1)

            def scores(i, k, h):
                if h < 4:
                    pe.wait_ge(stacked[k % 2][h], dma_count(i, k, len(STACK_PARTS)))
                if past(i, k, 1) or h >= 2:
                    pe.wait_ge(logits_sb, count(i, k, HEADS, h - 1))
                for t in range(NT):
                    op = pe.matmul(halves(S[h % 2])[:, t, :], stacks[k % 2][0:STACK, h % 4, 0, h // 4, P * t:P * t + P],
                                   stacks[k % 2][0:STACK, h % 4, 1, h // 4, :], start=True, stop=True)
                op.then_inc(scores_ps, 1)

            def transpose_e(i, k, h):
                pe.wait_ge(e_sb, count(i, k, HEADS, h + 1))
                if past(i, k, 1) or h >= 1:
                    pe.wait_ge(eT_sb, count(i, k, HEADS, h))
                for j in range(NT):
                    for t in range(NT):
                        op = pe.transpose(halves(T)[:, j, P * t:P * t + P], e[:, h % RING, t, P * j:P * j + P], ident[:, :])
                op.then_inc(eT_ps, 1)

            def weigh_values(i, k, g):
                pe.wait_ge(eT_sb, count(i, k, HEADS, 4 * g + 4))
                if g == 0 and past(i, k, 1):
                    pe.wait_ge(y_sb, count(i, k))
                if g == 1:
                    pe.wait_ge(oT_sb, count(i, k, GROUPS, 1))
                for j in range(NT):
                    for r in range(4):
                        h = 4 * g + r
                        op = pe.matmul(halves(O)[HD * r:HD * r + HD, g, :], V[k % 2][:, j, HD * h:HD * h + HD], eT[:, h, j, :],
                                       start=(j == 0), stop=(j == NT - 1), tile_position=(0, HD * r))
                op.then_inc(av_ps, 1)

            def transpose_out(i, k):
                pe.wait_ge(oT_sb, count(i, k + 1, GROUPS))
                for t in range(NT):
                    for g in range(GROUPS):
                        op = pe.transpose(halves(O)[:, t, P * g:P * g + P], oT[:, g, P * t:P * t + P], ident[:, :])
                op.then_inc(on_ps, 1)

            def step(i, k):
                if has(i, k - 2):
                    project0(i, k - 2)
                if has(i, k - 1):
                    transpose_p0(i, k - 1)
                if has(i, k - 4):
                    transpose_e(i, k - 4, 3)
                    scores(i, k - 4, 6)
                if has(i, k - 3):
                    c_row(i, k - 3)
                if has(i, k - 4):
                    scores(i, k - 4, 7)
                if has(i, k - 2):
                    transpose_x1(i, k - 2)
                if has(i, k - 4):
                    transpose_e(i, k - 4, 4)
                    weigh_values(i, k - 4, 0)
                    transpose_e(i, k - 4, 5)
                if has(i, k):
                    key_row(i, k)
                if has(i, k - 3):
                    scores(i, k - 3, 0)
                if has(i, k - 1):
                    combine0(i, k - 1)
                if has(i, k - 3):
                    scores(i, k - 3, 1)
                if has(i, k - 4):
                    transpose_e(i, k - 4, 6)
                if has(i, k - 2):
                    keys(i, k - 2)
                if has(i, k - 3):
                    scores(i, k - 3, 2)
                if has(i, k - 4):
                    transpose_e(i, k - 4, 7)
                if has(i, k - 2):
                    queries(i, k - 2)
                if has(i, k - 3):
                    scores(i, k - 3, 3)
                    transpose_e(i, k - 3, 0)
                    scores(i, k - 3, 4)
                if has(i, k - 4):
                    weigh_values(i, k - 4, 1)
                if has(i, k - 3):
                    transpose_e(i, k - 3, 1)
                if has(i, k - 2):
                    node_values(i, k - 2)
                if has(i, k - 4):
                    transpose_out(i, k - 4)
                if has(i, k - 3):
                    scores(i, k - 3, 5)
                    transpose_e(i, k - 3, 2)
            over_graphs(pe, step)


DEPTH = 6
LOADS = (3, 3, 4, 4)

_INS = ["x", "adj", "L0_gnn_W_fc", "L0_gnn_b_fc", "L0_gnn_w_q", "L0_gnn_b_q", "L0_gnn_w_k", "L0_gnn_b_k",
        "L1_gnn_W_q", "L1_gnn_b_q", "L1_gnn_W_k", "L1_gnn_b_k", "L1_gnn_W_v", "L1_gnn_b_v", "L1_gnn_w_g", "L1_gnn_b_g"]


def kernel(**inputs):
    import numpy as np
    import concourse.bacc as bacc
    from concourse.bass_utils import run_bass_kernel_spmd

    nc = bacc.Bacc("TRN2", target_bir_lowering=False, num_devices=1)
    arrays, args = {}, []
    for name in _INS:
        a = np.ascontiguousarray(inputs[name]).reshape(np.shape(inputs[name]) or (1,))
        arrays[f"in_{name}"] = a
        args.append(nc.dram_tensor(f"in_{name}", a.shape, F32, kind="ExternalInput").ap())
    args.append(nc.dram_tensor("out", (BATCH, NODES, FEAT), F32, kind="ExternalOutput").ap())
    build(nc, *args)
    r = run_bass_kernel_spmd(nc, [arrays], core_ids=[0])
    return r.results[0]["out"]
```
